# Optimizing a Trainium2 kernel written in Bass

```python
import numpy as np
import jax
import jax.numpy as jnp

def _softmax(x, axis=-1):
    return jax.nn.softmax(x, axis=axis)

def _gelu(x):
    return jax.nn.gelu(x, approximate=True)

def _silu(x):
    return jax.nn.silu(x)

def _sigmoid(x):
    return jax.nn.sigmoid(x)

def _layernorm(x, axis=-1, eps=1e-05):
    m = jnp.mean(x, axis=axis, keepdims=True)
    v = jnp.var(x, axis=axis, keepdims=True)
    return (x - m) / jnp.sqrt(v + eps)

def _scatter_add(tgt, idx, src, axis=0):
    return tgt.at[idx].add(src)

def _segment_sum(src, seg, n):
    return jax.ops.segment_sum(src, seg, n)
kernel_name = 'mk_xattn_ffn_d1_seqx_r8_2f834d'

def setup_inputs(seed: int=0):
    np.random.seed(seed)
    _w = jnp.asarray

    def _rec_inputs():
        import jax
        import jax.numpy as jnp
        _rk = jax.random.key(seed)
        x = 7.22e-05 + 1 * jax.random.normal(jax.random.fold_in(_rk, 1), (32, 128, 128), jnp.float32)
        _lenS = 128 - jax.random.randint(jax.random.fold_in(_rk, 7), (32,), 0, max(1, 128 // 4) + 1, jnp.int32)
        _lenS2 = 128 - jax.random.randint(jax.random.fold_in(_rk, 8), (32,), 0, max(1, 128 // 4) + 1, jnp.int32)
        _ctx_1024P = jax.random.normal(jax.random.fold_in(_rk, 11), (32, 16, 128), jnp.float32)
        _ctx_1024c = jax.random.dirichlet(jax.random.fold_in(_rk, 511), 0.3 * jnp.ones((16,), jnp.float32), (32, 128))
        _ctx_1024t = jnp.einsum('bsk,bkd->bsd', _ctx_1024c, _ctx_1024P)
        _ctx_1024t = _ctx_1024t * jax.lax.rsqrt(jnp.mean(jnp.square(_ctx_1024t)) + 1e-12) * 0.953939
        ctx_1024 = 4.13588e-05 + 0.999923 * (_ctx_1024t + 0.3 * jax.random.normal(jax.random.fold_in(_rk, 611), (32, 128, 128), jnp.float32))
        return (x, ctx_1024)
    x, ctx_1024 = _rec_inputs()

    def _L0_xattn_setup():
        import jax, jax.numpy as jnp
        import numpy as np
        MODEL_DIM = 128
        H = 16
        DK = MODEL_DIM // H
        key = jax.random.key(seed)
        ks = jax.random.split(key, 11)
        B, S, D = (4, 256, MODEL_DIM)
        s = 1.0 / np.sqrt(D)
        inp = {'q': jax.random.normal(ks[0], (B, S, D), jnp.float32), 'k': jax.random.normal(ks[1], (B, S, D), jnp.float32), 'v': jax.random.normal(ks[2], (B, S, D), jnp.float32), 'wq_w': jax.random.normal(ks[3], (H, D, DK), jnp.float32) * s, 'wq_b': jax.random.normal(ks[4], (H, DK), jnp.float32) * s, 'wk_w': jax.random.normal(ks[5], (H, D, DK), jnp.float32) * s, 'wk_b': jax.random.normal(ks[6], (H, DK), jnp.float32) * s, 'wv_w': jax.random.normal(ks[7], (H, D, DK), jnp.float32) * s, 'wv_b': jax.random.normal(ks[8], (H, DK), jnp.float32) * s, 'wo_w': jax.random.normal(ks[9], (D, D), jnp.float32) * s, 'wo_b': jax.random.normal(ks[10], (D,), jnp.float32) * s}
        return inp
    _L0_xattn_all = _L0_xattn_setup()
    _L0_xattn_in = {k: v for k, v in _L0_xattn_all.items() if k in ('wq_w', 'wq_b', 'wk_w', 'wk_b', 'wv_w', 'wv_b', 'wo_w', 'wo_b')}
    del _L0_xattn_all

    def _L0_ffn_setup():
        import jax, jax.numpy as jnp
        import numpy as np
        B, S, D, F, E, R, K = (1, 64, 128, 512, 8, 16, 2)
        SCALING = 32.0 / 16.0
        EPS = 1e-06

        def _forward(x, norm_w, w1, w3, w2, gate_w, a1, b1, a3, b3, a2, b2):
            Bq, Sq, Dq = x.shape
            nx = x * jax.lax.rsqrt(jnp.mean(x * x, axis=-1, keepdims=True) + EPS) * norm_w
            t = nx.reshape(-1, Dq)
            probs = jax.nn.softmax(t @ gate_w.T, axis=-1)
            topw, topi = jax.lax.top_k(probs, K)
            topw = topw / jnp.sum(topw, axis=-1, keepdims=True)
            weights = jnp.sum(jax.nn.one_hot(topi, E, dtype=t.dtype) * topw[..., None], axis=1)
            base1 = t @ w1.T
            base3 = t @ w3.T
            h1 = base1[None] + SCALING * jnp.einsum('etr,efr->etf', jnp.einsum('td,erd->etr', t, a1), b1)
            h3 = base3[None] + SCALING * jnp.einsum('etr,efr->etf', jnp.einsum('td,erd->etr', t, a3), b3)
            act = jax.nn.silu(h1) * h3
            out_e = jnp.einsum('etf,df->etd', act, w2) + SCALING * jnp.einsum('etr,edr->etd', jnp.einsum('etf,erf->etr', act, a2), b2)
            out = jnp.einsum('te,etd->td', weights, out_e)
            return out.reshape(Bq, Sq, Dq)
        key = jax.random.key(seed)
        ks = jax.random.split(key, 12)
        w = lambda k, shape: jax.random.normal(k, shape, dtype=jnp.float32) * 0.02
        return {'x': jax.random.normal(ks[0], (B, S, D), dtype=jnp.float32), 'norm_w': jnp.ones((D,), jnp.float32), 'w1': w(ks[1], (F, D)), 'w3': w(ks[2], (F, D)), 'w2': w(ks[3], (D, F)), 'gate_w': w(ks[4], (E, D)), 'a1': w(ks[5], (E, R, D)), 'b1': w(ks[6], (E, F, R)), 'a3': w(ks[7], (E, R, D)), 'b3': w(ks[8], (E, F, R)), 'a2': w(ks[9], (E, R, F)), 'b2': w(ks[10], (E, D, R))}
    _L0_ffn_all = _L0_ffn_setup()
    _L0_ffn_in = {k: v for k, v in _L0_ffn_all.items() if k in ('norm_w', 'w1', 'w3', 'w2', 'gate_w', 'a1', 'b1', 'a3', 'b3', 'a2', 'b2')}
    del _L0_ffn_all
    return {'x': x, 'ctx_1024': ctx_1024, 'L0_xattn_wq_w': _L0_xattn_in['wq_w'], 'L0_xattn_wq_b': _L0_xattn_in['wq_b'], 'L0_xattn_wk_w': _L0_xattn_in['wk_w'], 'L0_xattn_wk_b': _L0_xattn_in['wk_b'], 'L0_xattn_wv_w': _L0_xattn_in['wv_w'], 'L0_xattn_wv_b': _L0_xattn_in['wv_b'], 'L0_xattn_wo_w': _L0_xattn_in['wo_w'], 'L0_xattn_wo_b': _L0_xattn_in['wo_b'], 'L0_ffn_norm_w': _L0_ffn_in['norm_w'], 'L0_ffn_w1': _L0_ffn_in['w1'], 'L0_ffn_w3': _L0_ffn_in['w3'], 'L0_ffn_w2': _L0_ffn_in['w2'], 'L0_ffn_gate_w': _L0_ffn_in['gate_w'], 'L0_ffn_a1': _L0_ffn_in['a1'], 'L0_ffn_b1': _L0_ffn_in['b1'], 'L0_ffn_a3': _L0_ffn_in['a3'], 'L0_ffn_b3': _L0_ffn_in['b3'], 'L0_ffn_a2': _L0_ffn_in['a2'], 'L0_ffn_b2': _L0_ffn_in['b2']}

def reference(x, ctx_1024, L0_xattn_wq_w, L0_xattn_wq_b, L0_xattn_wk_w, L0_xattn_wk_b, L0_xattn_wv_w, L0_xattn_wv_b, L0_xattn_wo_w, L0_xattn_wo_b, L0_ffn_norm_w, L0_ffn_w1, L0_ffn_w3, L0_ffn_w2, L0_ffn_gate_w, L0_ffn_a1, L0_ffn_b1, L0_ffn_a3, L0_ffn_b3, L0_ffn_a2, L0_ffn_b2):
    import jax
    import jax.numpy as jnp

    def _L0_xattn_ref(q, k, v, wq_w, wq_b, wk_w, wk_b, wv_w, wv_b, wo_w, wo_b):
        import jax, jax.numpy as jnp
        import numpy as np
        MODEL_DIM = 128
        H = 16
        DK = MODEL_DIM // H
        qh = jnp.einsum('bsd,hdk->bhsk', q, wq_w) + wq_b[None, :, None, :]
        kh = jnp.einsum('bsd,hdk->bhsk', k, wk_w) + wk_b[None, :, None, :]
        vh = jnp.einsum('bsd,hdk->bhsk', v, wv_w) + wv_b[None, :, None, :]
        scale = 1.0 / jnp.sqrt(jnp.asarray(DK, qh.dtype))
        scores = jnp.einsum('bhqk,bhsk->bhqs', qh, kh) * scale
        out = jnp.einsum('bhqs,bhsk->bhqk', scores, vh)
        out = jax.nn.softmax(out, axis=-1)
        B, Hh, S, Dk = out.shape
        heads = jnp.transpose(out, (0, 2, 1, 3)).reshape(B, S, Hh * Dk)
        return heads @ wo_w.T + wo_b

    def _L0_ffn_ref(x, norm_w, w1, w3, w2, gate_w, a1, b1, a3, b3, a2, b2):
        import jax, jax.numpy as jnp
        import numpy as np
        B, S, D, F, E, R, K = (1, 64, 128, 512, 8, 16, 2)
        SCALING = 32.0 / 16.0
        EPS = 1e-06

        def _forward(x, norm_w, w1, w3, w2, gate_w, a1, b1, a3, b3, a2, b2):
            Bq, Sq, Dq = x.shape
            nx = x * jax.lax.rsqrt(jnp.mean(x * x, axis=-1, keepdims=True) + EPS) * norm_w
            t = nx.reshape(-1, Dq)
            probs = jax.nn.softmax(t @ gate_w.T, axis=-1)
            topw, topi = jax.lax.top_k(probs, K)
            topw = topw / jnp.sum(topw, axis=-1, keepdims=True)
            weights = jnp.sum(jax.nn.one_hot(topi, E, dtype=t.dtype) * topw[..., None], axis=1)
            base1 = t @ w1.T
            base3 = t @ w3.T
            h1 = base1[None] + SCALING * jnp.einsum('etr,efr->etf', jnp.einsum('td,erd->etr', t, a1), b1)
            h3 = base3[None] + SCALING * jnp.einsum('etr,efr->etf', jnp.einsum('td,erd->etr', t, a3), b3)
            act = jax.nn.silu(h1) * h3
            out_e = jnp.einsum('etf,df->etd', act, w2) + SCALING * jnp.einsum('etr,edr->etd', jnp.einsum('etf,erf->etr', act, a2), b2)
            out = jnp.einsum('te,etd->td', weights, out_e)
            return out.reshape(Bq, Sq, Dq)
        return _forward(x, norm_w, w1, w3, w2, gate_w, a1, b1, a3, b3, a2, b2)
    x = x + _L0_xattn_ref(_layernorm(x, axis=-1), ctx_1024, ctx_1024, L0_xattn_wq_w, L0_xattn_wq_b, L0_xattn_wk_w, L0_xattn_wk_b, L0_xattn_wv_w, L0_xattn_wv_b, L0_xattn_wo_w, L0_xattn_wo_b)
    x = x + _L0_ffn_ref(_layernorm(x, axis=-1), L0_ffn_norm_w, L0_ffn_w1, L0_ffn_w3, L0_ffn_w2, L0_ffn_gate_w, L0_ffn_a1, L0_ffn_b1, L0_ffn_a3, L0_ffn_b3, L0_ffn_a2, L0_ffn_b2)
    return x

_drawn_inputs = setup_inputs


def setup_inputs(seed=0):
    import zlib

    import numpy as np

    out = dict(_drawn_inputs(seed))
    spreads = {'L0_ffn_norm_w': (1.0, 0.6)}
    factors = {'L0_ffn_w1': 4.477,
     'L0_ffn_w3': 4.335,
     'L0_ffn_w2': 4.325,
     'L0_ffn_gate_w': 8.0,
     'L0_ffn_a1': 8.0,
     'L0_ffn_b1': 8.0,
     'L0_ffn_a3': 8.0,
     'L0_ffn_b3': 8.0,
     'L0_ffn_a2': 8.0,
     'L0_ffn_b2': 8.0}
    for name, (base, spread) in spreads.items():
        noise = np.random.default_rng([zlib.crc32(name.encode()), seed]).standard_normal(out[name].shape)
        drawn = base * np.exp(spread * noise) if base else spread * noise
        out[name] = jnp.asarray(drawn.astype(out[name].dtype))
    for name, factor in factors.items():
        out[name] = (out[name] * factor).astype(out[name].dtype)
    return out
```

```python
from contextlib import ExitStack

import concourse.bass as bass
from concourse import mybir

F32 = mybir.dt.float32
F32R = mybir.dt.float32r
BF16 = mybir.dt.bfloat16
U32 = mybir.dt.uint32
ALU = mybir.AluOpType
ACT = mybir.ActivationFunctionType
AX_X = mybir.AxisListType.X

BATCH, SEQ, D = 32, 128, 128
HEADS, DK = 16, 8
FF, EXPERTS, RANK, TOP = 512, 8, 16, 2
ER = EXPERTS * RANK
P = 128
TILES = 4
BLK = TILES * SEQ
BLOCKS = BATCH // TILES
CHUNKS = FF // P
LN_EPS, RMS_EPS = 1e-5, 1e-6
LORA_SCALE = 32.0 / 16.0
STEPS = [(0, 0), (1, 0), (0, 1), (1, 1), (2, 0), (3, 0), (2, 1), (3, 1)]
ACT_RING = 4


class Signal:

    def __init__(self, sem, per_block):
        self.sem, self.per_block = sem, per_block

    def of(self, block, n=None):
        return block * self.per_block + (self.per_block if n is None else n)


def build_program(nc: bass.Bass, x, ctx_t, wq, wq_b, wkv, wkv_b, wo_t, wo_b, norm_w, gate_t, w1_t, w3_t,
                  w2_t, a1_t, a3_t, a2_t, b1, b3, b2, head_mask, identity, expert_iota, out):
    with ExitStack() as ctx:
        def sb(name, shape, dt=F32):
            return ctx.enter_context(nc.sbuf_tensor(name, shape, dt))

        def psum(name):
            return ctx.enter_context(nc.psum_tensor(name, [P, BLK], F32))

        def sem(name):
            return ctx.enter_context(nc.semaphore(name))

        def signal(name, per_block=1):
            return Signal(sem(name), per_block)

        wq_sb = sb("wq_sb", [P, P])
        wkv_sb = sb("wkv_sb", [P, 2 * P])
        wo_sb = sb("wo_sb", [P, D])
        bq_sb = sb("bq_sb", [P, 1])
        bkv_sb = sb("bkv_sb", [P, 2 * P])
        bo_sb = sb("bo_sb", [P, D])
        nw_sb = sb("nw_sb", [P, 1])
        mask_sb = sb("mask_sb", [P, P])
        ident = sb("ident", [P, P])
        ident_bf = sb("ident_bf", [P, P], BF16)
        iota_sb = sb("iota_sb", [P, EXPERTS])
        minus_half = sb("minus_half", [P, TILES])
        eps_ln = sb("eps_ln", [P, TILES])
        eps_rms = sb("eps_rms", [P, TILES])
        nw_raw = sb("nw_raw", [P, 1])
        carrier = sb("carrier", [P, 1])
        gate_raw = sb("gate_raw", [P, EXPERTS])
        gate_sb = sb("gate_sb", [P, P])
        w13_raw = sb("w13_raw", [P, 2, FF])
        w13 = [sb("w13_hi", [P, 2, FF], F32R), sb("w13_lo", [P, 2, FF], F32R)]
        a13_raw = sb("a13_raw", [P, 2, ER])
        a13 = [sb("a13_hi", [P, 2, ER], F32R), sb("a13_lo", [P, 2, ER], F32R)]
        b13_raw = sb("b13_raw", [P, 2, FF])
        b13 = [sb("b13_hi", [P, 2, FF], F32R), sb("b13_lo", [P, 2, FF], F32R)]
        w2a2_raw = sb("w2a2_raw", [P, CHUNKS, D + ER])
        w2a2 = [sb("w2a2_hi", [P, CHUNKS, D + ER], F32R), sb("w2a2_lo", [P, CHUNKS, D + ER], F32R)]
        b2_raw = sb("b2_raw", [P, D])
        b2_sb = sb("b2_sb", [P, D])

        x_in = sb("x_in", [P, TILES, D])
        ctx_in = sb("ctx_in", [P, BLK])
        stats = sb("stats", [P, TILES, 6])
        mv = sb("mv", [P, TILES, 2])
        var_eps = sb("var_eps", [P, TILES])
        rstd = sb("rstd", [P, TILES])
        xn = sb("xn", [P, TILES, D])
        x_bias = sb("x_bias", [P, TILES, D])
        xn_t = sb("xn_t", [P, BLK])
        kv = sb("kv", [P, TILES, 2 * P])
        q_t = sb("q_t", [P, BLK])
        ktv = sb("ktv", [P, TILES, P])
        top_o = sb("top_o", [P, TILES * HEADS])
        e_o = sb("e_o", [P, TILES * HEADS, DK])
        sum_o = sb("sum_o", [P, TILES * HEADS])
        rec_o = sb("rec_o", [P, TILES * HEADS])
        heads = sb("heads", [P, TILES, P])
        heads_t = sb("heads_t", [P, BLK])
        x1 = sb("x1", [P, TILES, D])
        stats2 = sb("stats2", [P, TILES, 6])
        mv2 = sb("mv2", [P, TILES, 2])
        var_eps2 = sb("var_eps2", [P, TILES])
        rstd2 = sb("rstd2", [P, TILES])
        tok = sb("tok", [P, TILES, D])
        tok_t = sb("tok_t", [P, BLK])
        t_split = [sb("t_hi", [P, BLK], F32R), sb("t_lo", [P, BLK], F32R)]
        logits = sb("logits", [P, TILES, EXPERTS])
        top_l = sb("top_l", [P, TILES, 8])
        top_i = sb("top_i", [P, TILES, 8], U32)
        gap = sb("gap", [P, TILES])
        e_gap = sb("e_gap", [P, TILES])
        den = sb("den", [P, TILES])
        w_new = sb("w_new", [P, TOP, TILES])
        onehot = sb("onehot", [P, TOP + 1, TILES, EXPERTS])
        spread = sb("spread", [P, TOP, TILES, EXPERTS, RANK], BF16)
        masks = sb("masks", [P, TOP, BLK])
        u_hi = sb("u_hi", [P, 2, BLK], F32R)
        u_lo = sb("u_lo", [P, 2, BLK], F32R)
        um = [[sb(f"um{k}_{part}", [P, 2, BLK], F32R) for part in ("hi", "lo")] for k in range(TOP)]
        w_use = sb("w_use", [P, TOP, TILES])
        w_onehot = sb("w_onehot", [P, TOP, TILES, EXPERTS])
        res = sb("res", [P, TILES, D])
        th = sb("th", [P, 2, BLK])
        gated = sb("gated", [P, 2, BLK])
        act = sb("act", [P, ACT_RING, BLK])
        act_hi = sb("act_hi", [P, TOP, CHUNKS, BLK], F32R)
        act_lo = sb("act_lo", [P, TOP, CHUNKS, BLK], F32R)
        y = sb("y", [P, TILES, D])
        v_sum = sb("v_sum", [P, TILES, ER])
        v_one = sb("v_one", [P, 2, ER])
        v_t = sb("v_t", [P, BLK])

        h1_ps = [psum("h1_ps0"), psum("h1_ps1")]
        h3_ps = [psum("h3_ps0"), psum("h3_ps1")]
        ov_ps = [psum("ov_ps0"), psum("ov_ps1")]
        even_ps, odd_ps = psum("even_ps"), psum("odd_ps")

        attn_w_in = sem("attn_w_in")
        lora_w_in = sem("lora_w_in")
        hidden_w_in = sem("hidden_w_in")
        down_w_in = sem("down_w_in")
        const_pool = sem("const_pool")
        ident_bf_ready = sem("ident_bf_ready")
        gate_zero = sem("gate_zero")
        nw_ready = sem("nw_ready")
        small_w_ready = sem("small_w_ready")
        w_hi_ready = sem("w_hi_ready")
        w_lo_ready = sem("w_lo_ready")
        x_loaded = signal("x_loaded", 16)
        ctx_loaded = signal("ctx_loaded", 16)
        stats_done = signal("stats_done")
        mv_done = signal("mv_done")
        var_done = signal("var_done")
        rstd_done = signal("rstd_done")
        xn_done = signal("xn_done")
        x_bias_done = signal("x_bias_done")
        xn_t_mm = signal("xn_t_mm")
        xn_t_done = signal("xn_t_done")
        kv_mm = signal("kv_mm", 2)
        kv_done = signal("kv_done", 2)
        q_mm = signal("q_mm")
        q_t_done = signal("q_t_done")
        ktv_mm = signal("ktv_mm")
        ktv_done = signal("ktv_done")
        o_mm = signal("o_mm")
        top_o_done = signal("top_o_done")
        o_shifted = signal("o_shifted")
        o_exp = signal("o_exp")
        sum_o_done = signal("sum_o_done")
        rec_o_done = signal("rec_o_done")
        heads_done = signal("heads_done")
        heads_t_mm = signal("heads_t_mm")
        heads_t_done = signal("heads_t_done")
        wo_mm = signal("wo_mm")
        x1_done = signal("x1_done")
        stats2_done = signal("stats2_done")
        mv2_done = signal("mv2_done")
        var2_done = signal("var2_done")
        rstd2_done = signal("rstd2_done")
        tok_done = signal("tok_done")
        tok_t_mm = signal("tok_t_mm")
        tok_t_done = signal("tok_t_done")
        t_hi_done = signal("t_hi_done")
        t_lo_done = signal("t_lo_done")
        logits_mm = signal("logits_mm")
        logits_done = signal("logits_done")
        top_l_done = signal("top_l_done")
        top_i_done = signal("top_i_done")
        gap_done = signal("gap_done")
        e_gap_done = signal("e_gap_done")
        den_done = signal("den_done")
        w0_done = signal("w0_done")
        w1_done = signal("w1_done")
        onehot_done = signal("onehot_done")
        onehot_diff = signal("onehot_diff")
        spread_done = signal("spread_done", TOP)
        masks_mm = signal("masks_mm", TOP)
        masks_done = signal("masks_done", TOP)
        u_mm = signal("u_mm", 2)
        u_hi_done = signal("u_hi_done", 2)
        u_lo_done = signal("u_lo_done", 2)
        um_first = signal("um_first")
        um_diff = signal("um_diff")
        handed_over = signal("handed_over")
        res_done = signal("res_done")
        h1_mm = signal("h1_mm", len(STEPS))
        h3_mm = signal("h3_mm", len(STEPS))
        th_done = signal("th_done", len(STEPS))
        gated_done = signal("gated_done", len(STEPS))
        act_done = signal("act_done", len(STEPS))
        act_hi_done = signal("act_hi_done", len(STEPS))
        act_lo_done = signal("act_lo_done", len(STEPS))
        ov_mm = signal("ov_mm", 4)
        ov_read = signal("ov_read", 4)
        v_sum_done = signal("v_sum_done", 2)
        v_t_mm = signal("v_t_mm")
        v_t_done = signal("v_t_done")
        y_mm = signal("y_mm")
        y_done = signal("y_done")
        stored = signal("stored", 16)

        def tile4(ap):
            return ap[:].rearrange("p (t d) -> p t d", t=TILES)

        def as_f32(ap):
            return ap.bitcast(F32)

        def all_iterations(eng, iteration):
            iteration(0, tail=False, late=True, early=True)
            with eng.Fori(1, BLOCKS - 2) as b:
                iteration(b, tail=True, late=True, early=True)
            iteration(BLOCKS - 2, tail=True, late=True, early=False)
            iteration(BLOCKS - 1, tail=True, late=False, early=False)

        block = ctx.enter_context(nc.Block())

        @block.sync
        def _(sp):
            def load(n, first=False):
                if not first:
                    sp.wait_ge(xn_done.sem, xn_done.of(n - 1))
                    sp.wait_ge(x_bias_done.sem, x_bias_done.of(n - 1))
                sp.dma_start(x_in[:].rearrange("p t d -> p (t d)"), x[:, bass.ds(n * BLK, BLK)]).then_inc(x_loaded.sem, 16)
                if not first:
                    sp.wait_ge(kv_mm.sem, kv_mm.of(n - 1))
                sp.dma_start(ctx_in[:], ctx_t[:, bass.ds(n * BLK, BLK)]).then_inc(ctx_loaded.sem, 16)

            def store(n):
                sp.wait_ge(y_done.sem, y_done.of(n))
                sp.dma_start(out[:, bass.ds(n * BLK, BLK)], y[:].rearrange("p t d -> p (t d)")).then_inc(stored.sem, 16)

            load(0, first=True)
            sp.dma_start(wq_sb[:], wq).then_inc(attn_w_in, 16)
            sp.dma_start(wkv_sb[:], wkv).then_inc(attn_w_in, 16)
            sp.dma_start(ident[:], identity).then_inc(attn_w_in, 16)
            sp.dma_start(bkv_sb[:], wkv_b.partition_broadcast(P)).then_inc(attn_w_in, 16)
            sp.dma_start(wo_sb[:], wo_t).then_inc(attn_w_in, 16)
            sp.dma_start(w13_raw[:, 0, :], w1_t).then_inc(hidden_w_in, 16)
            sp.dma_start(w13_raw[:, 1, :], w3_t).then_inc(hidden_w_in, 16)
            sp.dma_start(b13_raw[:, 0, :], b1).then_inc(hidden_w_in, 16)
            sp.dma_start(b13_raw[:, 1, :], b3).then_inc(hidden_w_in, 16)
            load(1)

            def iteration(b, tail, late, early):
                if early:
                    load(b + 2)
                if tail:
                    store(b - 1)

            all_iterations(sp, iteration)
            store(BLOCKS - 1)
            sp.wait_ge(stored.sem, stored.of(BLOCKS - 1))

        ATTN_W_IN, LORA_W_IN, HIDDEN_W_IN, DOWN_W_IN = 9 * 16, 4 * 16, 4 * 16, 3 * 16

        @block.tensor
        def _(pe):
            def early_half(n, first=False):
                pe.wait_ge(xn_done.sem, xn_done.of(n))
                if not first:
                    pe.wait_ge(masks_done.sem, masks_done.of(n - 1, 1))
                for t in range(TILES):
                    mm = nc.tensor.transpose(even_ps[:, t * P:(t + 1) * P], xn[:, t, :], ident[:])
                mm.then_inc(xn_t_mm.sem, 1)
                yield
                pe.wait_ge(ctx_loaded.sem, ctx_loaded.of(n))
                for half in range(2):
                    if half == 0:
                        if not first:
                            pe.wait_ge(masks_done.sem, masks_done.of(n - 1))
                    else:
                        pe.wait_ge(xn_t_done.sem, xn_t_done.of(n))
                    bank = (odd_ps, even_ps)[half]
                    for j in range(2):
                        t = 2 * half + j
                        mm = nc.tensor.matmul(bank[:, j * 2 * P:(j + 1) * 2 * P], ctx_in[:, t * SEQ:(t + 1) * SEQ],
                                              wkv_sb[:], start=True, stop=True)
                    mm.then_inc(kv_mm.sem, 1)
                    yield
                pe.wait_ge(kv_done.sem, kv_done.of(n, 1))
                nc.tensor.matmul(odd_ps[:], wq_sb[:], xn_t[:], start=True, stop=True).then_inc(q_mm.sem, 1)
                yield
                pe.wait_ge(kv_done.sem, kv_done.of(n))
                for t in range(TILES):
                    mm = nc.tensor.matmul(even_ps[:, t * P:(t + 1) * P], kv[:, t, 0:P], kv[:, t, P:2 * P],
                                          start=True, stop=True)
                mm.then_inc(ktv_mm.sem, 1)
                yield
                pe.wait_ge(q_t_done.sem, q_t_done.of(n))
                pe.wait_ge(ktv_done.sem, ktv_done.of(n))
                for t in range(TILES):
                    mm = nc.tensor.matmul(odd_ps[:, t * P:(t + 1) * P], q_t[:, t * P:(t + 1) * P], ktv[:, t, :],
                                          start=True, stop=True)
                mm.then_inc(o_mm.sem, 1)
                yield

            def late_half(n, after_tail=False):
                pe.wait_ge(heads_done.sem, heads_done.of(n))
                for t in range(TILES):
                    mm = nc.tensor.transpose(even_ps[:, t * P:(t + 1) * P], heads[:, t, :], ident[:])
                mm.then_inc(heads_t_mm.sem, 1)
                yield
                pe.wait_ge(heads_t_done.sem, heads_t_done.of(n))
                if after_tail:
                    pe.wait_ge(y_done.sem, y_done.of(n - 2))
                for t in range(TILES):
                    mm = nc.tensor.matmul(odd_ps[:, t * P:(t + 1) * P], heads_t[:, t * P:(t + 1) * P], wo_sb[:],
                                          start=True, stop=True)
                mm.then_inc(wo_mm.sem, 1)
                yield
                pe.wait_ge(tok_done.sem, tok_done.of(n))
                for t in range(TILES):
                    mm = nc.tensor.transpose(even_ps[:, t * P:(t + 1) * P], tok[:, t, :], ident[:])
                mm.then_inc(tok_t_mm.sem, 1)
                yield
                pe.wait_ge(tok_t_done.sem, tok_t_done.of(n))
                for t in range(TILES):
                    mm = nc.tensor.matmul(odd_ps[:, t * P:(t + 1) * P], tok_t[:, t * P:(t + 1) * P], gate_sb[:],
                                          start=True, stop=True)
                mm.then_inc(logits_mm.sem, 1)
                yield
                pe.wait_ge(t_lo_done.sem, t_lo_done.of(n))
                for s, bank in ((0, even_ps), (1, odd_ps)):
                    if s == 1:
                        pe.wait_ge(logits_done.sem, logits_done.of(n))
                    for i, (w, m) in enumerate(((0, 0), (0, 1), (1, 0))):
                        mm = nc.tensor.matmul(bank[:], a13[w][:, s, :], t_split[m][:], start=(i == 0), stop=(i == 2))
                    mm.then_inc(u_mm.sem, 1)
                    yield
                for k, bank in ((0, even_ps), (1, odd_ps)):
                    pe.wait_ge(u_hi_done.sem, u_hi_done.of(n, k + 1))
                    pe.wait_ge(u_lo_done.sem, u_lo_done.of(n, k + 1))
                    pe.wait_ge(spread_done.sem, spread_done.of(n, k + 1))
                    for t in range(TILES):
                        mm = nc.tensor.matmul(bank[:, t * P:(t + 1) * P],
                                              spread[:, k, t].rearrange("p e r -> p (e r)"), ident_bf[:],
                                              start=True, stop=True)
                    mm.then_inc(masks_mm.sem, 1)
                    yield

            def hidden(b, n, first):
                c, k = STEPS[n]
                cols = slice(c * P, (c + 1) * P)
                if n == 0:
                    pe.wait_ge(um_first.sem, um_first.of(b))
                if n == 2:
                    pe.wait_ge(um_diff.sem, um_diff.of(b))
                for s, banks, free, done in ((0, h1_ps, gated_done, h1_mm), (1, h3_ps, act_done, h3_mm)):
                    if n >= 2:
                        pe.wait_ge(free.sem, free.of(b, n - 1))
                    elif not first:
                        pe.wait_ge(free.sem, free.of(b - 1, len(STEPS) + n - 1))
                    terms = [(b13[w], um[k][m][:, s, :]) for w, m in ((0, 0), (0, 1), (1, 0))]
                    if k == 0:
                        terms = [(w13[w], t_split[m][:]) for w, m in ((0, 0), (0, 1), (1, 0))] + terms
                    for i, (w, m) in enumerate(terms):
                        mm = nc.tensor.matmul(banks[n % 2][:], w[:, s, cols], m, start=(k == 0 and i == 0),
                                              stop=(i == len(terms) - 1), skip_group_check=True)
                    mm.then_inc(done.sem, 1)

            def down(b, k, t, first):
                half = t // 2
                if t == 0:
                    last = [n for n, step in enumerate(STEPS) if step[1] == k][-1]
                    pe.wait_ge(act_lo_done.sem, act_lo_done.of(b, last + 1))
                if t % 2 == 0:
                    if k == 1:
                        pe.wait_ge(ov_read.sem, ov_read.of(b, half + 1))
                    elif not first:
                        pe.wait_ge(ov_read.sem, ov_read.of(b - 1, half + 3))
                rows = slice(t * P, (t + 1) * P)
                width = D + ER
                dst = ov_ps[half][:, (t % 2) * width:(t % 2 + 1) * width]
                for c in range(CHUNKS):
                    for a, w in ((act_hi, 0), (act_hi, 1), (act_lo, 0)):
                        mm = nc.tensor.matmul(dst, a[:, k, c, rows], w2a2[w][:, c, :],
                                              start=(c == 0 and a is act_hi and w == 0),
                                              stop=(c == CHUNKS - 1 and a is act_lo))
                if t % 2 == 1:
                    mm.then_inc(ov_mm.sem, 1)

            def tail_transpose(b):
                pe.wait_ge(v_sum_done.sem, v_sum_done.of(b))
                for t in range(TILES):
                    mm = nc.tensor.transpose(even_ps[:, t * P:(t + 1) * P], v_sum[:, t, :], ident[:])
                mm.then_inc(v_t_mm.sem, 1)

            def tail_product(b, after_early):
                pe.wait_ge(v_t_done.sem, v_t_done.of(b))
                if after_early:
                    pe.wait_ge(o_shifted.sem, o_shifted.of(b + 2))
                for t in range(TILES):
                    mm = nc.tensor.matmul(odd_ps[:, t * P:(t + 1) * P], v_t[:, t * P:(t + 1) * P], b2_sb[:],
                                          start=True, stop=True)
                mm.then_inc(y_mm.sem, 1)

            def iteration(b, tail, late, early):
                first = not tail
                late_steps = late_half(b + 1, after_tail=tail) if late else iter(())
                early_steps = early_half(b + 2) if early else iter(())
                hidden(b, 0, first)
                if tail:
                    tail_transpose(b - 1)
                hidden(b, 1, first)
                if tail:
                    tail_product(b - 1, after_early=late)
                hidden(b, 2, first)
                next(late_steps, None)
                hidden(b, 3, first)
                next(late_steps, None)
                hidden(b, 4, first)
                hidden(b, 5, first)
                next(late_steps, None)
                hidden(b, 6, first)
                next(late_steps, None)
                next(late_steps, None)
                hidden(b, 7, first)
                next(late_steps, None)
                down(b, 0, 0, first)
                down(b, 0, 1, first)
                next(late_steps, None)
                down(b, 0, 2, first)
                next(late_steps, None)
                down(b, 0, 3, first)
                next(early_steps, None)
                down(b, 1, 0, first)
                next(early_steps, None)
                down(b, 1, 1, first)
                next(early_steps, None)
                next(early_steps, None)
                down(b, 1, 2, first)
                next(early_steps, None)
                down(b, 1, 3, first)
                next(early_steps, None)
                next(late_steps, None)
                next(early_steps, None)

            pe.wait_ge(attn_w_in, ATTN_W_IN)
            for _ in early_half(0, first=True):
                pass
            pe.wait_ge(small_w_ready, 2)
            pe.wait_ge(ident_bf_ready, 1)
            pe.wait_ge(w_hi_ready, 4)
            pe.wait_ge(w_lo_ready, 4)
            for _ in late_half(0):
                pass
            for _ in early_half(1):
                pass
            all_iterations(pe, iteration)
            tail_transpose(BLOCKS - 1)
            tail_product(BLOCKS - 1, after_early=False)

        @block.scalar
        def _(sc):
            def early_xn_t(n):
                sc.wait_ge(xn_t_mm.sem, xn_t_mm.of(n))
                nc.scalar.copy(xn_t[:], even_ps[:]).then_inc(xn_t_done.sem, 1)

            def early_q(n):
                sc.wait_ge(q_mm.sem, q_mm.of(n))
                nc.scalar.activation(q_t[:], odd_ps[:], ACT.Identity, bias=bq_sb[:, 0:1]).then_inc(q_t_done.sem, 1)

            def late_exp(n):
                sc.wait_ge(o_shifted.sem, o_shifted.of(n))
                nc.scalar.activation(e_o[:], e_o[:], ACT.Exp).then_inc(o_exp.sem, 1)

            def late_heads_t(n):
                sc.wait_ge(heads_t_mm.sem, heads_t_mm.of(n))
                nc.scalar.copy(heads_t[:], even_ps[:]).then_inc(heads_t_done.sem, 1)

            def late_tok_t(n):
                sc.wait_ge(tok_t_mm.sem, tok_t_mm.of(n))
                nc.scalar.copy(tok_t[:], even_ps[:]).then_inc(tok_t_done.sem, 1)
                nc.scalar.copy(t_split[0][:], even_ps[:]).then_inc(t_hi_done.sem, 1)

            def late_gap(n):
                sc.wait_ge(gap_done.sem, gap_done.of(n))
                nc.scalar.activation(e_gap[:], gap[:], ACT.Exp).then_inc(e_gap_done.sem, 1)

            def late_u_hi(n, s):
                sc.wait_ge(u_mm.sem, u_mm.of(n, s + 1))
                nc.scalar.copy(u_hi[:, s, :], (even_ps, odd_ps)[s][:]).then_inc(u_hi_done.sem, 1)

            def late_spread(n, k):
                done = (onehot_done, onehot_diff)[k]
                sc.wait_ge(done.sem, done.of(n))
                src = onehot[:, 2 * k].unsqueeze(3).to_broadcast([P, TILES, EXPERTS, RANK])
                nc.scalar.copy(spread[:, k], src).then_inc(spread_done.sem, 1)

            def late_mask(n, k):
                sc.wait_ge(masks_mm.sem, masks_mm.of(n, k + 1))
                nc.scalar.copy(masks[:, k, :], (even_ps, odd_ps)[k][:]).then_inc(masks_done.sem, 1)

            def residual(b, first):
                sc.wait_ge(x1_done.sem, x1_done.of(b))
                if not first:
                    sc.wait_ge(ov_read.sem, ov_read.of(b - 1, 2))
                nc.scalar.copy(res[:], x1[:]).then_inc(res_done.sem, 1)

            def tanh(b, n):
                sc.wait_ge(h1_mm.sem, h1_mm.of(b, n + 1))
                nc.scalar.activation(th[:, n % 2, :], h1_ps[n % 2][:], ACT.Tanh, scale=0.5).then_inc(th_done.sem, 1)

            def high(b, n):
                c, k = STEPS[n]
                sc.wait_ge(act_done.sem, act_done.of(b, n + 1))
                nc.scalar.copy(act_hi[:, k, c, :], act[:, n % ACT_RING, :]).then_inc(act_hi_done.sem, 1)

            def iteration(b, tail, late, early):
                residual(b, first=not tail)
                tanh(b, 0)
                if late:
                    late_exp(b + 1)
                if tail:
                    sc.wait_ge(v_t_mm.sem, v_t_mm.of(b - 1))
                    nc.scalar.copy(v_t[:], even_ps[:]).then_inc(v_t_done.sem, 1)
                high(b, 0)
                tanh(b, 1)
                high(b, 1)
                tanh(b, 2)
                if late:
                    late_heads_t(b + 1)
                high(b, 2)
                tanh(b, 3)
                high(b, 3)
                tanh(b, 4)
                high(b, 4)
                tanh(b, 5)
                if late:
                    late_tok_t(b + 1)
                high(b, 5)
                tanh(b, 6)
                if late:
                    late_u_hi(b + 1, 0)
                    late_gap(b + 1)
                high(b, 6)
                tanh(b, 7)
                if late:
                    late_u_hi(b + 1, 1)
                high(b, 7)
                if late:
                    late_spread(b + 1, 0)
                    late_spread(b + 1, 1)
                    late_mask(b + 1, 0)
                    late_mask(b + 1, 1)
                if early:
                    early_xn_t(b + 2)
                    early_q(b + 2)

            sc.dma_start(bq_sb[:], wq_b).then_inc(attn_w_in, 16)
            sc.dma_start(bo_sb[:], wo_b.partition_broadcast(P)).then_inc(attn_w_in, 16)
            sc.dma_start(mask_sb[:], head_mask).then_inc(attn_w_in, 16)
            sc.dma_start(iota_sb[:], expert_iota.partition_broadcast(P)).then_inc(attn_w_in, 16)
            sc.dma_start(nw_raw[:], norm_w).then_inc(lora_w_in, 16)
            sc.dma_start(gate_raw[:], gate_t).then_inc(lora_w_in, 16)
            sc.dma_start(a13_raw[:, 0, :], a1_t).then_inc(lora_w_in, 16)
            sc.dma_start(a13_raw[:, 1, :], a3_t).then_inc(lora_w_in, 16)
            sc.dma_start(w2a2_raw[:, :, 0:D], w2_t.rearrange("(c p) d -> p c d", p=P)).then_inc(down_w_in, 16)
            sc.dma_start(w2a2_raw[:, :, D:D + ER], a2_t.rearrange("(c p) e -> p c e", p=P)).then_inc(down_w_in, 16)
            sc.dma_start(b2_raw[:], b2).then_inc(down_w_in, 16)
            sc.wait_ge(attn_w_in, ATTN_W_IN)
            early_xn_t(0)
            early_q(0)
            sc.wait_ge(nw_ready, 1)
            sc.wait_ge(lora_w_in, LORA_W_IN)
            nc.scalar.activation(a13[0][:], a13_raw[:], ACT.Identity, scale=nw_sb[:, 0:1]).then_inc(w_hi_ready, 1)
            sc.wait_ge(hidden_w_in, HIDDEN_W_IN)
            nc.scalar.activation(w13[0][:], w13_raw[:], ACT.Identity, scale=nw_sb[:, 0:1]).then_inc(w_hi_ready, 1)
            nc.scalar.activation(b13[0][:], b13_raw[:], ACT.Identity, scale=LORA_SCALE).then_inc(w_hi_ready, 1)
            sc.wait_ge(down_w_in, DOWN_W_IN)
            nc.scalar.activation(w2a2[0][:], w2a2_raw[:], ACT.Identity, scale=0.5).then_inc(w_hi_ready, 1)
            late_exp(0)
            late_heads_t(0)
            late_tok_t(0)
            late_u_hi(0, 0)
            late_gap(0)
            late_u_hi(0, 1)
            late_spread(0, 0)
            late_spread(0, 1)
            late_mask(0, 0)
            late_mask(0, 1)
            early_xn_t(1)
            early_q(1)
            all_iterations(sc, iteration)
            sc.wait_ge(v_t_mm.sem, v_t_mm.of(BLOCKS - 1))
            nc.scalar.copy(v_t[:], even_ps[:]).then_inc(v_t_done.sem, 1)

        @block.vector
        def _(ve):
            def normalise(dst, src, mean_var, rs, rstd_sig, n, done):
                ve.wait_ge(rstd_sig.sem, rstd_sig.of(n))
                for t in range(TILES):
                    op = nc.vector.tensor_scalar(dst[:, t, :], src[:, t, :], mean_var[:, t, 0:1], rs[:, t:t + 1],
                                                 ALU.subtract, ALU.mult)
                op.then_inc(done.sem, 1)

            def moments(src, st, mean_var, st_sig, mv_sig, n):
                for t in range(TILES):
                    op = nc.vector.bn_stats(st[:, t, :], src[:, t, :])
                op.then_inc(st_sig.sem, 1)
                ve.wait_ge(st_sig.sem, st_sig.of(n))
                nc.vector.memset(carrier[:], 0.0)
                for t in range(TILES):
                    op = nc.vector.bn_aggr(mean_var[:, t, :], st[:, t, :])
                op.then_inc(mv_sig.sem, 1)

            def early_moments(n):
                ve.wait_ge(x_loaded.sem, x_loaded.of(n))
                moments(x_in, stats, mv, stats_done, mv_done, n)

            def early_xn(n):
                normalise(xn, x_in, mv, rstd, rstd_done, n, xn_done)

            def early_kv(n, half):
                ve.wait_ge(kv_mm.sem, kv_mm.of(n, half + 1))
                bank = (odd_ps, even_ps)[half]
                nc.vector.tensor_tensor(kv[:, 2 * half:2 * half + 2, :], bank[:].rearrange("p (t d) -> p t d", t=2),
                                        bkv_sb[:].unsqueeze(1).to_broadcast([P, 2, 2 * P]), ALU.add)\
                    .then_inc(kv_done.sem, 1)

            def early_ktv(n):
                ve.wait_ge(ktv_mm.sem, ktv_mm.of(n))
                nc.vector.tensor_tensor(ktv[:], tile4(even_ps), mask_sb[:].unsqueeze(1).to_broadcast([P, TILES, P]),
                                        ALU.mult).then_inc(ktv_done.sem, 1)

            def late_shift(n):
                ve.wait_ge(o_mm.sem, o_mm.of(n))
                o = odd_ps[:].rearrange("p (g k) -> p g k", k=DK)
                nc.vector.tensor_reduce(top_o[:], o, AX_X, ALU.max).then_inc(top_o_done.sem, 1)
                ve.wait_ge(top_o_done.sem, top_o_done.of(n))
                nc.vector.tensor_tensor(e_o[:], o, top_o[:].unsqueeze(2).to_broadcast([P, TILES * HEADS, DK]),
                                        ALU.subtract).then_inc(o_shifted.sem, 1)

            def late_sum(n):
                ve.wait_ge(o_exp.sem, o_exp.of(n))
                nc.vector.tensor_reduce(sum_o[:], e_o[:], AX_X, ALU.add).then_inc(sum_o_done.sem, 1)
                ve.wait_ge(sum_o_done.sem, sum_o_done.of(n))
                nc.vector.reciprocal(rec_o[:], sum_o[:]).then_inc(rec_o_done.sem, 1)

            def late_x1(n, first=False):
                ve.wait_ge(wo_mm.sem, wo_mm.of(n))
                ve.wait_ge(x_bias_done.sem, x_bias_done.of(n))
                if not first:
                    ve.wait_ge(res_done.sem, res_done.of(n - 1))
                nc.vector.tensor_tensor(x1[:], tile4(odd_ps), x_bias[:], ALU.add).then_inc(x1_done.sem, 1)
                ve.wait_ge(x1_done.sem, x1_done.of(n))
                moments(x1, stats2, mv2, stats2_done, mv2_done, n)

            def late_tok(n):
                normalise(tok, x1, mv2, rstd2, rstd2_done, n, tok_done)

            def late_t_lo(n):
                ve.wait_ge(tok_t_done.sem, tok_t_done.of(n))
                ve.wait_ge(t_hi_done.sem, t_hi_done.of(n))
                nc.vector.tensor_tensor(t_split[1][:], tok_t[:], as_f32(t_split[0][:]), ALU.subtract)\
                    .then_inc(t_lo_done.sem, 1)

            def late_gate(n):
                ve.wait_ge(logits_mm.sem, logits_mm.of(n))
                nc.vector.tensor_copy(logits[:], tile4(odd_ps)[:, :, 0:EXPERTS]).then_inc(logits_done.sem, 1)
                ve.wait_ge(logits_done.sem, logits_done.of(n))
                nc.vector.memset(carrier[:], 0.0)
                for t in range(TILES):
                    op = nc.vector.max(top_l[:, t, :], logits[:, t, :])
                op.then_inc(top_l_done.sem, 1)
                ve.wait_ge(top_l_done.sem, top_l_done.of(n))
                nc.vector.tensor_tensor(gap[:], top_l[:, :, 1], top_l[:, :, 0], ALU.subtract).then_inc(gap_done.sem, 1)
                for t in range(TILES):
                    op = nc.vector.max_index(top_i[:, t, :], top_l[:, t, :], logits[:, t, :])
                op.then_inc(top_i_done.sem, 1)
                ve.wait_ge(top_i_done.sem, top_i_done.of(n))
                for k in range(TOP):
                    op = nc.vector.tensor_tensor(onehot[:, k], iota_sb[:].unsqueeze(1).to_broadcast([P, TILES, EXPERTS]),
                                                 top_i[:, :, k:k + 1].to_broadcast([P, TILES, EXPERTS]), ALU.is_equal)
                op.then_inc(onehot_done.sem, 1)
                ve.wait_ge(onehot_done.sem, onehot_done.of(n))
                nc.vector.tensor_tensor(onehot[:, 2], onehot[:, 1], onehot[:, 0], ALU.subtract)\
                    .then_inc(onehot_diff.sem, 1)

            def late_weights(n):
                ve.wait_ge(e_gap_done.sem, e_gap_done.of(n))
                nc.vector.tensor_scalar(den[:], e_gap[:], 1.0, None, ALU.add).then_inc(den_done.sem, 1)
                ve.wait_ge(den_done.sem, den_done.of(n))
                nc.vector.reciprocal(w_new[:, 0, :], den[:]).then_inc(w0_done.sem, 1)
                ve.wait_ge(w0_done.sem, w0_done.of(n))
                nc.vector.tensor_tensor(w_new[:, 1, :], e_gap[:], w_new[:, 0, :], ALU.mult).then_inc(w1_done.sem, 1)

            def late_u_lo(n, s):
                ve.wait_ge(u_hi_done.sem, u_hi_done.of(n, s + 1))
                nc.vector.tensor_tensor(u_lo[:, s, :], (even_ps, odd_ps)[s][:], as_f32(u_hi[:, s, :]), ALU.subtract)\
                    .then_inc(u_lo_done.sem, 1)

            def late_um_first(n):
                ve.wait_ge(masks_done.sem, masks_done.of(n, 1))
                ve.wait_ge(u_lo_done.sem, u_lo_done.of(n))
                mask = masks[:, 0:1, :].to_broadcast([P, 2, BLK])
                nc.vector.tensor_tensor(um[0][0][:], as_f32(u_hi[:]), mask, ALU.mult)
                nc.vector.tensor_tensor(um[0][1][:], as_f32(u_lo[:]), mask, ALU.mult).then_inc(um_first.sem, 1)

            def hand_over(b):
                ve.wait_ge(w1_done.sem, w1_done.of(b))
                nc.vector.tensor_copy(w_use[:], w_new[:])
                nc.vector.tensor_tensor(w_onehot[:], onehot[:, 0:TOP],
                                        w_new[:].unsqueeze(3).to_broadcast([P, TOP, TILES, EXPERTS]), ALU.mult)\
                    .then_inc(handed_over.sem, 1)

            def gate_step(b, n):
                ve.wait_ge(th_done.sem, th_done.of(b, n + 1))
                nc.vector.scalar_tensor_tensor(out=gated[:, n % 2, :], in0=th[:, n % 2, :], scalar=1.0,
                                               in1=h1_ps[n % 2][:], op0=ALU.add, op1=ALU.mult)\
                    .then_inc(gated_done.sem, 1)
                ve.wait_ge(h3_mm.sem, h3_mm.of(b, n + 1))
                ve.wait_ge(gated_done.sem, gated_done.of(b, n + 1))
                if n >= ACT_RING:
                    ve.wait_ge(act_lo_done.sem, act_lo_done.of(b, n - ACT_RING + 1))
                nc.vector.tensor_tensor(act[:, n % ACT_RING, :], gated[:, n % 2, :], h3_ps[n % 2][:], ALU.mult)\
                    .then_inc(act_done.sem, 1)

            def collect(b, k, half, first=False):
                ve.wait_ge(ov_mm.sem, ov_mm.of(b, 2 * k + half + 1))
                bank = ov_ps[half][:].rearrange("p (j c) -> p j c", j=2)
                tiles = slice(2 * half, 2 * half + 2)
                if k == 0 and half == 0:
                    ve.wait_ge(handed_over.sem, handed_over.of(b))
                    ve.wait_ge(res_done.sem, res_done.of(b))
                    if not first:
                        ve.wait_ge(stored.sem, stored.of(b - 1))
                if k == 1:
                    ve.wait_ge(ov_read.sem, ov_read.of(b, half + 1))
                    if half == 1:
                        ve.wait_ge(v_sum_done.sem, v_sum_done.of(b, 1))
                for j in range(2):
                    t = 2 * half + j
                    nc.vector.scalar_tensor_tensor(out=y[:, t, :], in0=bank[:, j, 0:D], scalar=w_use[:, k, t:t + 1],
                                                   in1=(res if k == 0 else y)[:, t, :], op0=ALU.mult, op1=ALU.add)
                nc.vector.tensor_tensor((v_sum[:, tiles, :] if k == 0 else v_one[:]).rearrange("p j (e r) -> p j e r", r=RANK),
                                        bank[:, :, D:D + ER].rearrange("p j (e r) -> p j e r", r=RANK),
                                        w_onehot[:, k, tiles].unsqueeze(3).to_broadcast([P, 2, EXPERTS, RANK]),
                                        ALU.mult).then_inc(ov_read.sem, 1)
                if k == 1:
                    ve.wait_ge(ov_read.sem, ov_read.of(b, half + 3))
                    nc.vector.tensor_tensor(v_sum[:, tiles, :], v_sum[:, tiles, :], v_one[:], ALU.add)\
                        .then_inc(v_sum_done.sem, 1)

            def finish(b):
                ve.wait_ge(y_mm.sem, y_mm.of(b))
                ve.wait_ge(v_sum_done.sem, v_sum_done.of(b))
                nc.vector.tensor_tensor(y[:], y[:], tile4(odd_ps), ALU.add).then_inc(y_done.sem, 1)

            def iteration(b, tail, late, early):
                if tail:
                    collect(b - 1, 1, 1)
                hand_over(b)
                if late:
                    late_shift(b + 1)
                gate_step(b, 0)
                if late:
                    late_sum(b + 1)
                gate_step(b, 1)
                if tail:
                    finish(b - 1)
                gate_step(b, 2)
                gate_step(b, 3)
                if late:
                    late_x1(b + 1)
                gate_step(b, 4)
                if late:
                    late_tok(b + 1)
                gate_step(b, 5)
                if late:
                    late_t_lo(b + 1)
                gate_step(b, 6)
                if late:
                    late_gate(b + 1)
                    late_u_lo(b + 1, 0)
                gate_step(b, 7)
                if late:
                    late_u_lo(b + 1, 1)
                    late_weights(b + 1)
                if early:
                    early_moments(b + 2)
                collect(b, 0, 0, first=not tail)
                if early:
                    early_xn(b + 2)
                if late:
                    late_um_first(b + 1)
                collect(b, 0, 1, first=not tail)
                if early:
                    early_kv(b + 2, 0)
                    early_kv(b + 2, 1)
                collect(b, 1, 0)
                if early:
                    early_ktv(b + 2)

            nc.vector.memset(gate_sb[:], 0.0).then_inc(gate_zero, 1)
            early_moments(0)
            early_xn(0)
            ve.wait_ge(attn_w_in, ATTN_W_IN)
            nc.vector.tensor_copy(ident_bf[:], ident[:]).then_inc(ident_bf_ready, 1)
            early_kv(0, 0)
            early_kv(0, 1)
            early_ktv(0)
            late_shift(0)
            ve.wait_ge(lora_w_in, LORA_W_IN)
            nc.vector.tensor_scalar(nw_sb[:], nw_raw[:], (1.0 + RMS_EPS) ** -0.5, None, ALU.mult).then_inc(nw_ready, 1)
            ve.wait_ge(gate_zero, 1)
            ve.wait_ge(nw_ready, 1)
            nc.vector.tensor_scalar(gate_sb[:, 0:EXPERTS], gate_raw[:], nw_sb[:, 0:1], None, ALU.mult)\
                .then_inc(small_w_ready, 1)

            def low(i, split, raw, scale):
                ve.wait_ge(w_hi_ready, i + 1)
                nc.vector.scalar_tensor_tensor(out=split[1][:], in0=raw[:], scalar=scale, in1=as_f32(split[0][:]),
                                               op0=ALU.mult, op1=ALU.subtract).then_inc(w_lo_ready, 1)

            low(0, a13, a13_raw, nw_sb[:, 0:1])
            ve.wait_ge(hidden_w_in, HIDDEN_W_IN)
            low(1, w13, w13_raw, nw_sb[:, 0:1])
            low(2, b13, b13_raw, LORA_SCALE)
            ve.wait_ge(down_w_in, DOWN_W_IN)
            low(3, w2a2, w2a2_raw, 0.5)
            nc.vector.tensor_scalar(b2_sb[:], b2_raw[:], LORA_SCALE, None, ALU.mult).then_inc(small_w_ready, 1)
            late_sum(0)
            late_x1(0, first=True)
            late_tok(0)
            late_t_lo(0)
            late_gate(0)
            late_u_lo(0, 0)
            late_u_lo(0, 1)
            late_weights(0)
            late_um_first(0)
            early_moments(1)
            early_xn(1)
            early_kv(1, 0)
            early_kv(1, 1)
            early_ktv(1)
            all_iterations(ve, iteration)
            collect(BLOCKS - 1, 1, 1)
            finish(BLOCKS - 1)

        @block.gpsimd
        def _(pool):
            def inverse_root(src, var_out, rs, mv_sig, var_sig, rstd_sig, n, eps):
                pool.wait_ge(mv_sig.sem, mv_sig.of(n))
                nc.gpsimd.tensor_tensor(var_out[:], src[:, :, 1], eps[:], ALU.add).then_inc(var_sig.sem, 1)
                pool.wait_ge(var_sig.sem, var_sig.of(n))
                nc.gpsimd.tensor_tensor(rs[:], var_out[:], minus_half[:], ALU.pow).then_inc(rstd_sig.sem, 1)

            def early_rstd(n):
                inverse_root(mv, var_eps, rstd, mv_done, var_done, rstd_done, n, eps_ln)

            def early_bias(n, first=False):
                pool.wait_ge(x_loaded.sem, x_loaded.of(n))
                if not first:
                    pool.wait_ge(x1_done.sem, x1_done.of(n - 1))
                nc.gpsimd.tensor_tensor(x_bias[:], x_in[:], bo_sb[:].unsqueeze(1).to_broadcast([P, TILES, D]), ALU.add)\
                    .then_inc(x_bias_done.sem, 1)

            def late_heads(n):
                pool.wait_ge(rec_o_done.sem, rec_o_done.of(n))
                nc.gpsimd.tensor_tensor(heads[:].rearrange("p t (h k) -> p (t h) k", k=DK), e_o[:],
                                        rec_o[:].unsqueeze(2).to_broadcast([P, TILES * HEADS, DK]), ALU.mult)\
                    .then_inc(heads_done.sem, 1)

            def late_rstd(n):
                inverse_root(mv2, var_eps2, rstd2, mv2_done, var2_done, rstd2_done, n, eps_rms)

            def late_um_diff(n):
                pool.wait_ge(masks_done.sem, masks_done.of(n))
                pool.wait_ge(u_lo_done.sem, u_lo_done.of(n))
                mask = masks[:, 1:2, :].to_broadcast([P, 2, BLK])
                nc.gpsimd.tensor_tensor(um[1][0][:], as_f32(u_hi[:]), mask, ALU.mult)
                nc.gpsimd.tensor_tensor(um[1][1][:], as_f32(u_lo[:]), mask, ALU.mult).then_inc(um_diff.sem, 1)

            def low(b, n):
                c, k = STEPS[n]
                pool.wait_ge(act_hi_done.sem, act_hi_done.of(b, n + 1))
                nc.gpsimd.tensor_tensor(act_lo[:, k, c, :], act[:, n % ACT_RING, :], as_f32(act_hi[:, k, c, :]),
                                        ALU.subtract).then_inc(act_lo_done.sem, 1)

            def iteration(b, tail, late, early):
                low(b, 0)
                if late:
                    late_heads(b + 1)
                low(b, 1)
                low(b, 2)
                low(b, 3)
                if late:
                    late_rstd(b + 1)
                low(b, 4)
                low(b, 5)
                low(b, 6)
                low(b, 7)
                if early:
                    early_rstd(b + 2)
                    early_bias(b + 2)
                if late:
                    late_um_diff(b + 1)

            nc.gpsimd.memset(eps_ln[:], LN_EPS)
            nc.gpsimd.memset(eps_rms[:], LN_EPS * RMS_EPS / (1.0 + RMS_EPS))
            nc.gpsimd.memset(minus_half[:], -0.5).then_inc(const_pool, 1)
            pool.wait_ge(const_pool, 1)
            early_rstd(0)
            pool.wait_ge(attn_w_in, ATTN_W_IN)
            early_bias(0, first=True)
            late_heads(0)
            late_rstd(0)
            late_um_diff(0)
            early_rstd(1)
            early_bias(1)
            all_iterations(pool, iteration)


_OUT = "out_dram"


def kernel(**inputs):
    import numpy as np
    import concourse.bacc as bacc
    from concourse.bass_utils import run_bass_kernel_spmd

    a = {k: np.asarray(v) for k, v in inputs.items()}
    at, ff = (lambda n: a["L0_xattn_" + n]), (lambda n: a["L0_ffn_" + n])

    def heads_side_by_side(w):
        return w.transpose(1, 0, 2).reshape(D, HEADS * DK)

    arrays = {
        "x": a["x"].transpose(1, 0, 2).reshape(SEQ, BATCH * D),
        "ctx_t": a["ctx_1024"].transpose(2, 0, 1).reshape(D, BATCH * SEQ),
        "wq": heads_side_by_side(at("wq_w")),
        "wq_b": at("wq_b").reshape(HEADS * DK, 1),
        "wkv": np.concatenate([heads_side_by_side(at("wk_w")), heads_side_by_side(at("wv_w"))], axis=1),
        "wkv_b": np.concatenate([at("wk_b").reshape(-1), at("wv_b").reshape(-1)]),
        "wo_t": at("wo_w").T,
        "wo_b": at("wo_b"),
        "norm_w": ff("norm_w").reshape(D, 1),
        "gate_t": ff("gate_w").T,
        "w1_t": ff("w1").T, "w3_t": ff("w3").T, "w2_t": ff("w2").T,
        "a1_t": ff("a1").reshape(ER, D).T, "a3_t": ff("a3").reshape(ER, D).T,
        "a2_t": ff("a2").reshape(ER, FF).T,
        "b1": ff("b1").transpose(0, 2, 1).reshape(ER, FF), "b3": ff("b3").transpose(0, 2, 1).reshape(ER, FF),
        "b2": ff("b2").transpose(0, 2, 1).reshape(ER, D),
        "head_mask": np.kron(np.eye(HEADS), np.ones((DK, DK))).astype(np.float32) * np.float32(DK ** -0.5),
        "identity": np.eye(P, dtype=np.float32),
        "expert_iota": np.arange(EXPERTS, dtype=np.float32),
    }
    nc = bacc.Bacc("TRN2", target_bir_lowering=False, num_devices=1)
    feed, args = {}, []
    for name, value in arrays.items():
        value = np.ascontiguousarray(value)
        feed[f"in_{name}_dram"] = value
        args.append(nc.dram_tensor(f"in_{name}_dram", value.shape, mybir.dt.from_np(value.dtype), kind="ExternalInput").ap())
    args.append(nc.dram_tensor(_OUT, (SEQ, BATCH * D), F32, kind="ExternalOutput").ap())
    build_program(nc, *args)
    r = run_bass_kernel_spmd(nc, [feed], core_ids=[0])
    return r.results[0][_OUT].reshape(SEQ, BATCH, D).transpose(1, 0, 2)
```

```python
from contextlib import ExitStack

import concourse.bass as bass
from concourse import mybir

F32 = mybir.dt.float32
F32R = mybir.dt.float32r
BF16 = mybir.dt.bfloat16
U32 = mybir.dt.uint32
ALU = mybir.AluOpType
ACT = mybir.ActivationFunctionType
AX_X = mybir.AxisListType.X

BATCH, SEQ, D = 32, 128, 128
HEADS, DK = 16, 8
FF, EXPERTS, RANK, TOP = 512, 8, 16, 2
ER = EXPERTS * RANK
P = 128
TILES = 4
BLK = TILES * SEQ
BLOCKS = BATCH // TILES
CHUNKS = FF // P
LN_EPS, RMS_EPS = 1e-5, 1e-6
LORA_SCALE = 32.0 / 16.0
STEPS = [(0, 0), (1, 0), (0, 1), (1, 1), (2, 0), (3, 0), (2, 1), (3, 1)]
SILU_RING = 4
AHEAD = 2
TERMS = ((0, 0), (0, 1), (1, 0))


class Signal:

    def __init__(self, sem, per_block):
        self.sem, self.per_block = sem, per_block

    def of(self, block, n=None):
        return block * self.per_block + (self.per_block if n is None else n)


def build_program(nc: bass.Bass, x, ctx_t, wq, wq_b, wkv, wkv_b, wo_t, wo_b, norm_w, gate_t, w1_t, w3_t,
                  w2_t, a1_t, a3_t, a2_t, b1, b3, b2, head_mask, identity, expert_iota, out):
    with ExitStack() as ctx:
        def sb(name, shape, dt=F32):
            return ctx.enter_context(nc.sbuf_tensor(name, shape, dt))

        def psum(name):
            return ctx.enter_context(nc.psum_tensor(name, [P, BLK], F32))

        def sem(name):
            return ctx.enter_context(nc.semaphore(name))

        def signal(name, per_block=1):
            return Signal(sem(name), per_block)

        wq_sb = sb("wq_sb", [P, P])
        wkv_sb = sb("wkv_sb", [P, 2 * P])
        wkv_split = [sb("wkv_hi", [P, 2 * P], F32R), sb("wkv_lo", [P, 2 * P], F32R)]
        wo_sb = sb("wo_sb", [P, D])
        bq_sb = sb("bq_sb", [P, 1])
        bkv_sb = sb("bkv_sb", [P, 2 * P])
        bo_sb = sb("bo_sb", [P, D])
        nw_sb = sb("nw_sb", [P, 1])
        mask_sb = sb("mask_sb", [P, P])
        ident = sb("ident", [P, P])
        ident_bf = sb("ident_bf", [P, P], BF16)
        iota_sb = sb("iota_sb", [P, EXPERTS])
        minus_half = sb("minus_half", [P, TILES])
        eps_ln = sb("eps_ln", [P, TILES])
        eps_rms = sb("eps_rms", [P, TILES])
        nw_raw = sb("nw_raw", [P, 1])
        carrier = sb("carrier", [P, 1])
        gate_raw = sb("gate_raw", [P, EXPERTS])
        gate_sb = sb("gate_sb", [P, P])
        w13_raw = sb("w13_raw", [P, 2, FF])
        w13 = [sb("w13_hi", [P, 2, FF], F32R), sb("w13_lo", [P, 2, FF], F32R)]
        a13_raw = sb("a13_raw", [P, 2, ER])
        a13 = [sb("a13_hi", [P, 2, ER], F32R), sb("a13_lo", [P, 2, ER], F32R)]
        b13_raw = sb("b13_raw", [P, 2, FF])
        b13 = [sb("b13_hi", [P, 2, FF], F32R), sb("b13_lo", [P, 2, FF], F32R)]
        w2a2_raw = sb("w2a2_raw", [P, CHUNKS, D + ER])
        w2a2 = [sb("w2a2_hi", [P, CHUNKS, D + ER], F32R), sb("w2a2_lo", [P, CHUNKS, D + ER], F32R)]
        b2_raw = sb("b2_raw", [P, D])
        b2_split = [sb("b2_hi", [P, D], F32R), sb("b2_lo", [P, D], F32R)]

        x_in = sb("x_in", [P, TILES, D])
        ctx_in = sb("ctx_in", [P, BLK])
        ctx_split = [sb("ctx_hi", [P, BLK], F32R), sb("ctx_lo", [P, BLK], F32R)]
        stats = sb("stats", [P, TILES, 6])
        mv = sb("mv", [P, TILES, 2])
        var_eps = sb("var_eps", [P, TILES])
        rstd = sb("rstd", [P, TILES])
        xn = sb("xn", [P, TILES, D])
        x_bias = sb("x_bias", [P, TILES, D])
        xn_t = sb("xn_t", [P, BLK])
        kv = sb("kv", [P, TILES, 2 * P])
        q_t = sb("q_t", [P, BLK])
        ktv = sb("ktv", [P, TILES, P])
        top_o = sb("top_o", [P, TILES * HEADS])
        e_o = sb("e_o", [P, TILES * HEADS, DK])
        sum_o = sb("sum_o", [P, TILES * HEADS])
        rec_o = sb("rec_o", [P, TILES * HEADS])
        heads = sb("heads", [P, TILES, P])
        heads_t = sb("heads_t", [P, BLK])
        x1 = sb("x1", [P, TILES, D])
        stats2 = sb("stats2", [P, TILES, 6])
        mv2 = sb("mv2", [P, TILES, 2])
        var_eps2 = sb("var_eps2", [P, TILES])
        rstd2 = sb("rstd2", [P, TILES])
        tok = sb("tok", [P, TILES, D])
        tok_t = sb("tok_t", [P, BLK])
        t_split = [sb("t_hi", [P, BLK], F32R), sb("t_lo", [P, BLK], F32R)]
        logits = sb("logits", [P, TILES, EXPERTS])
        top_l = sb("top_l", [P, TILES, 8])
        top_i = sb("top_i", [P, TILES, 8], U32)
        gap = sb("gap", [P, TILES])
        e_gap = sb("e_gap", [P, TILES])
        den = sb("den", [P, TILES])
        w_new = sb("w_new", [P, TILES])
        wide_ratio = sb("wide_ratio", [P, TILES, P])
        ratio = sb("ratio", [P, BLK])
        onehot = sb("onehot", [P, TOP + 1, TILES, EXPERTS])
        spread = sb("spread", [P, TOP, TILES, EXPERTS, RANK], BF16)
        masks = sb("masks", [P, TOP, BLK])
        u_hi = sb("u_hi", [P, 2, BLK], F32R)
        u_lo = sb("u_lo", [P, 2, BLK], F32R)
        um = [[sb(f"um{k}_{part}", [P, 2, BLK], F32R) for part in ("hi", "lo")] for k in range(TOP)]
        w_use = sb("w_use", [P, TILES])
        res = sb("res", [P, TILES, D])
        silu = sb("silu", [P, SILU_RING, BLK])
        act_first = sb("act_first", [P, CHUNKS, BLK])
        act_second = sb("act_second", [P, 2, BLK])
        scaled = sb("scaled", [P, CHUNKS, BLK])
        total = sb("total", [P, CHUNKS, BLK])
        b_split = [sb("b_hi", [P, CHUNKS, BLK], F32R), sb("b_lo", [P, CHUNKS, BLK], F32R)]
        z_split = [sb("z_hi", [P, CHUNKS, BLK], F32R), sb("z_lo", [P, CHUNKS, BLK], F32R)]
        v_parts = sb("v_parts", [P, 2, BLK])
        v = sb("v", [P, BLK])
        v_split = [sb("v_hi", [P, BLK], F32R), sb("v_lo", [P, BLK], F32R)]
        o_t = sb("o_t", [P, BLK])
        y = sb("y", [P, TILES, D])

        h1_ps = [psum("h1_ps0"), psum("h1_ps1")]
        h3_ps = [psum("h3_ps0"), psum("h3_ps1")]
        z_ps, b_ps = psum("z_ps"), psum("b_ps")
        even_ps, odd_ps = psum("even_ps"), psum("odd_ps")

        ident_in = sem("ident_in")
        qkv_w_in = sem("qkv_w_in")
        attn_w_in = sem("attn_w_in")
        lora_w_in = sem("lora_w_in")
        hidden_w_in = sem("hidden_w_in")
        down_w_in = sem("down_w_in")
        const_pool = sem("const_pool")
        ident_bf_ready = sem("ident_bf_ready")
        gate_zero = sem("gate_zero")
        nw_ready = sem("nw_ready")
        gate_w_ready = sem("gate_w_ready")
        w_hi_ready = sem("w_hi_ready")
        w_lo_ready = sem("w_lo_ready")
        x_loaded = signal("x_loaded", 16)
        ctx_loaded = signal("ctx_loaded", 16)
        stats_done = signal("stats_done")
        mv_done = signal("mv_done")
        var_done = signal("var_done")
        rstd_done = signal("rstd_done")
        xn_done = signal("xn_done")
        x_bias_done = signal("x_bias_done")
        ctx_hi_done = signal("ctx_hi_done")
        ctx_lo_done = signal("ctx_lo_done")
        xn_t_mm = signal("xn_t_mm")
        xn_t_done = signal("xn_t_done")
        kv_mm = signal("kv_mm", 2)
        kv_done = signal("kv_done", 2)
        q_mm = signal("q_mm")
        q_t_done = signal("q_t_done")
        ktv_mm = signal("ktv_mm")
        ktv_done = signal("ktv_done")
        o_mm = signal("o_mm")
        top_o_done = signal("top_o_done")
        o_shifted = signal("o_shifted")
        o_exp = signal("o_exp")
        sum_o_done = signal("sum_o_done")
        rec_o_done = signal("rec_o_done")
        heads_done = signal("heads_done")
        heads_t_mm = signal("heads_t_mm")
        heads_t_done = signal("heads_t_done")
        wo_mm = signal("wo_mm")
        x1_done = signal("x1_done")
        stats2_done = signal("stats2_done")
        mv2_done = signal("mv2_done")
        var2_done = signal("var2_done")
        rstd2_done = signal("rstd2_done")
        tok_done = signal("tok_done")
        tok_t_mm = signal("tok_t_mm")
        tok_t_done = signal("tok_t_done")
        t_hi_done = signal("t_hi_done")
        t_lo_done = signal("t_lo_done")
        logits_mm = signal("logits_mm")
        logits_done = signal("logits_done")
        top_l_done = signal("top_l_done")
        top_i_done = signal("top_i_done")
        gap_done = signal("gap_done")
        e_gap_done = signal("e_gap_done")
        den_done = signal("den_done")
        w0_done = signal("w0_done")
        wide_ratio_done = signal("wide_ratio_done")
        ratio_mm = signal("ratio_mm")
        ratio_done = signal("ratio_done")
        onehot_done = signal("onehot_done")
        onehot_diff = signal("onehot_diff")
        spread_done = signal("spread_done", TOP)
        masks_mm = signal("masks_mm", TOP)
        masks_done = signal("masks_done", TOP)
        u_mm = signal("u_mm", 2)
        u_hi_done = signal("u_hi_done", 2)
        u_lo_done = signal("u_lo_done", 2)
        um_first = signal("um_first", 2)
        um_diff = signal("um_diff")
        handed_over = signal("handed_over")
        res_done = signal("res_done")
        h1_mm = signal("h1_mm", len(STEPS))
        h3_mm = signal("h3_mm", len(STEPS))
        silu_done = signal("silu_done", len(STEPS))
        act_done = signal("act_done", len(STEPS))
        scaled_done = signal("scaled_done", CHUNKS)
        total_done = signal("total_done", CHUNKS)
        b_hi_done = signal("b_hi_done", CHUNKS)
        b_lo_done = signal("b_lo_done", CHUNKS)
        z_hi_done = signal("z_hi_done", CHUNKS)
        z_lo_done = signal("z_lo_done", CHUNKS)
        a2z_mm = signal("a2z_mm")
        a2b_mm = signal("a2b_mm")
        v_part_done = signal("v_part_done", 2)
        v_done = signal("v_done")
        v_hi_done = signal("v_hi_done")
        v_lo_done = signal("v_lo_done")
        o_t_mm = signal("o_t_mm")
        o_t_done = signal("o_t_done")
        y_mm = signal("y_mm")
        y_done = signal("y_done")
        stored = signal("stored", 16)

        def tile4(ap):
            return ap[:].rearrange("p (t d) -> p t d", t=TILES)

        def as_f32(ap):
            return ap.bitcast(F32)

        def all_iterations(eng, iteration):
            iteration(0, tail_too=False, late=True, early=True)
            with eng.Fori(1, BLOCKS - 2) as b:
                iteration(b, tail_too=True, late=True, early=True)
            iteration(BLOCKS - 2, tail_too=True, late=True, early=False)
            iteration(BLOCKS - 1, tail_too=True, late=False, early=False)

        block = ctx.enter_context(nc.Block())

        @block.sync
        def _(sp):
            def load(n):
                sp.wait_ge(xn_done.sem, xn_done.of(n - 1))
                sp.wait_ge(x_bias_done.sem, x_bias_done.of(n - 1))
                sp.dma_start(x_in[:].rearrange("p t d -> p (t d)"), x[:, bass.ds(n * BLK, BLK)]).then_inc(x_loaded.sem, 16)
                if isinstance(n, int) and n <= AHEAD:
                    sp.wait_ge(kv_mm.sem, kv_mm.of(n - 1))
                else:
                    sp.wait_ge(ctx_lo_done.sem, ctx_lo_done.of(n - 1 - AHEAD))
                sp.dma_start(ctx_in[:], ctx_t[:, bass.ds(n * BLK, BLK)]).then_inc(ctx_loaded.sem, 16)

            def store(n):
                sp.wait_ge(y_done.sem, y_done.of(n))
                sp.dma_start(out[:, bass.ds(n * BLK, BLK)], y[:].rearrange("p t d -> p (t d)")).then_inc(stored.sem, 16)

            sp.dma_start(x_in[:].rearrange("p t d -> p (t d)"), x[:, 0:BLK]).then_inc(x_loaded.sem, 16)
            sp.dma_start(wkv_sb[:], wkv).then_inc(qkv_w_in, 16)
            sp.dma_start(ident[:], identity).then_inc(ident_in, 16)
            sp.dma_start(wq_sb[:], wq).then_inc(qkv_w_in, 16)
            sp.dma_start(mask_sb[:], head_mask).then_inc(attn_w_in, 16)
            sp.dma_start(wo_sb[:], wo_t).then_inc(attn_w_in, 16)
            sp.dma_start(w13_raw[:, 0, :], w1_t).then_inc(hidden_w_in, 16)
            sp.dma_start(w13_raw[:, 1, :], w3_t).then_inc(hidden_w_in, 16)
            load(1)
            sp.dma_start(w2a2_raw[:, :, 0:D], w2_t.rearrange("(c p) d -> p c d", p=P)).then_inc(down_w_in, 16)
            sp.dma_start(w2a2_raw[:, :, D:D + ER], a2_t.rearrange("(c p) e -> p c e", p=P)).then_inc(down_w_in, 16)
            sp.dma_start(b2_raw[:], b2).then_inc(down_w_in, 16)

            def iteration(b, tail_too, late, early):
                if early:
                    load(b + 2)
                if tail_too:
                    store(b - 1)

            all_iterations(sp, iteration)
            store(BLOCKS - 1)
            sp.wait_ge(stored.sem, stored.of(BLOCKS))

        QKV_W_IN, ATTN_W_IN, LORA_W_IN, HIDDEN_W_IN, DOWN_W_IN = 4 * 16, 3 * 16, 5 * 16, 4 * 16, 3 * 16

        @block.tensor
        def _(pe):
            def turn(dst, src):
                for t in range(TILES):
                    mm = nc.tensor.transpose(dst[:, t * P:(t + 1) * P], src[:, t, :], ident[:])
                return mm

            def by_tile(dst, stationary, moving):
                for t in range(TILES):
                    mm = nc.tensor.matmul(dst[:, t * P:(t + 1) * P], stationary(t), moving(t), start=True, stop=True)
                return mm

            def turn_x(n, bank):
                pe.wait_ge(xn_done.sem, xn_done.of(n))
                turn(bank, xn).then_inc(xn_t_mm.sem, 1)

            def keys_values_ahead(n, half, bank):
                pe.wait_ge(ctx_loaded.sem, ctx_loaded.of(n))
                for j in range(2):
                    t = 2 * half + j
                    mm = nc.tensor.matmul(bank[:, j * 2 * P:(j + 1) * 2 * P], ctx_in[:, t * SEQ:(t + 1) * SEQ],
                                          wkv_sb[:], start=True, stop=True)
                mm.then_inc(kv_mm.sem, 1)

            def keys_values(n, half, bank):
                pe.wait_ge(ctx_hi_done.sem, ctx_hi_done.of(n - AHEAD))
                pe.wait_ge(ctx_lo_done.sem, ctx_lo_done.of(n - AHEAD))
                for j in range(2):
                    t = 2 * half + j
                    for i, (w, m) in enumerate(TERMS):
                        mm = nc.tensor.matmul(bank[:, j * 2 * P:(j + 1) * 2 * P], ctx_split[m][:, t * SEQ:(t + 1) * SEQ],
                                              wkv_split[w][:], start=(i == 0), stop=(i == 2))
                mm.then_inc(kv_mm.sem, 1)

            def queries(n, bank):
                pe.wait_ge(xn_t_done.sem, xn_t_done.of(n))
                nc.tensor.matmul(bank[:], wq_sb[:], xn_t[:], start=True, stop=True).then_inc(q_mm.sem, 1)

            def keys_times_values(n, bank):
                pe.wait_ge(kv_done.sem, kv_done.of(n))
                by_tile(bank, lambda t: kv[:, t, 0:P], lambda t: kv[:, t, P:2 * P]).then_inc(ktv_mm.sem, 1)

            def attention_out(n, bank):
                pe.wait_ge(q_t_done.sem, q_t_done.of(n))
                pe.wait_ge(ktv_done.sem, ktv_done.of(n))
                by_tile(bank, lambda t: q_t[:, t * P:(t + 1) * P], lambda t: ktv[:, t, :]).then_inc(o_mm.sem, 1)

            def early_ahead(n, ktv_bank, o_bank, x_early):
                keys_values_ahead(n, 0, h3_ps[0])
                yield
                if x_early:
                    turn_x(n, h1_ps[0])
                    yield
                keys_values_ahead(n, 1, h3_ps[1])
                yield
                if not x_early:
                    turn_x(n, h1_ps[0])
                    yield
                queries(n, h1_ps[1])
                yield
                keys_times_values(n, ktv_bank)
                yield
                attention_out(n, o_bank)
                yield

            def early_half(n):
                pe.wait_ge(u_hi_done.sem, u_hi_done.of(n - 1, 1))
                pe.wait_ge(u_lo_done.sem, u_lo_done.of(n - 1, 1))
                turn_x(n, odd_ps)
                yield
                pe.wait_ge(u_hi_done.sem, u_hi_done.of(n - 1))
                pe.wait_ge(u_lo_done.sem, u_lo_done.of(n - 1))
                keys_values(n, 0, even_ps)
                yield
                pe.wait_ge(xn_t_done.sem, xn_t_done.of(n))
                keys_values(n, 1, odd_ps)
                yield
                pe.wait_ge(kv_done.sem, kv_done.of(n, 1))
                queries(n, even_ps)
                yield
                pe.wait_ge(q_t_done.sem, q_t_done.of(n))
                pe.wait_ge(masks_done.sem, masks_done.of(n - 1))
                keys_times_values(n, even_ps)
                yield
                pe.wait_ge(ratio_done.sem, ratio_done.of(n - 1))
                attention_out(n, odd_ps)
                yield

            def late_half(n, after_tail=False, after_ratio=False, after_early=False):
                pe.wait_ge(heads_done.sem, heads_done.of(n))
                if after_ratio:
                    pe.wait_ge(ratio_done.sem, ratio_done.of(n - 1))
                turn(odd_ps, heads).then_inc(heads_t_mm.sem, 1)
                yield
                pe.wait_ge(heads_t_done.sem, heads_t_done.of(n))
                if after_tail:
                    pe.wait_ge(y_done.sem, y_done.of(n - 2))
                by_tile(even_ps, lambda t: heads_t[:, t * P:(t + 1) * P], lambda t: wo_sb[:]).then_inc(wo_mm.sem, 1)
                yield
                pe.wait_ge(tok_done.sem, tok_done.of(n))
                turn(odd_ps, tok).then_inc(tok_t_mm.sem, 1)
                yield
                pe.wait_ge(tok_t_done.sem, tok_t_done.of(n))
                by_tile(even_ps, lambda t: tok_t[:, t * P:(t + 1) * P], lambda t: gate_sb[:]).then_inc(logits_mm.sem, 1)
                yield
                pe.wait_ge(t_hi_done.sem, t_hi_done.of(n))
                pe.wait_ge(t_lo_done.sem, t_lo_done.of(n))
                for s, bank in ((0, odd_ps), (1, even_ps)):
                    if s == 1:
                        pe.wait_ge(logits_done.sem, logits_done.of(n))
                    for i, (w, m) in enumerate(TERMS):
                        mm = nc.tensor.matmul(bank[:], a13[w][:, s, :], t_split[m][:], start=(i == 0), stop=(i == 2))
                    mm.then_inc(u_mm.sem, 1)
                    yield
                for k, bank in ((0, odd_ps), (1, even_ps)):
                    if not after_early:
                        pe.wait_ge(u_hi_done.sem, u_hi_done.of(n, k + 1))
                        pe.wait_ge(u_lo_done.sem, u_lo_done.of(n, k + 1))
                    elif k == 0:
                        pe.wait_ge(kv_done.sem, kv_done.of(n + 1))
                    else:
                        pe.wait_ge(q_t_done.sem, q_t_done.of(n + 1))
                    pe.wait_ge(spread_done.sem, spread_done.of(n, k + 1))
                    by_tile(bank, lambda t: spread[:, k, t].rearrange("p e r -> p (e r)"), lambda t: ident_bf[:])\
                        .then_inc(masks_mm.sem, 1)
                    yield
                pe.wait_ge(wide_ratio_done.sem, wide_ratio_done.of(n))
                pe.wait_ge(masks_done.sem, masks_done.of(n, 1))
                turn(odd_ps, wide_ratio).then_inc(ratio_mm.sem, 1)
                yield

            def hidden(b, n, first):
                c, k = STEPS[n]
                cols = slice(c * P, (c + 1) * P)
                for s, banks, free, done in ((0, h1_ps, silu_done, h1_mm), (1, h3_ps, act_done, h3_mm)):
                    if n >= 2:
                        pe.wait_ge(free.sem, free.of(b, n - 1))
                    elif not first:
                        pe.wait_ge(free.sem, free.of(b - 1, len(STEPS) + n - 1))
                    if k == 0:
                        for i, (w, m) in enumerate(TERMS):
                            nc.tensor.matmul(banks[n % 2][:], w13[w][:, s, cols], t_split[m][:], start=(i == 0),
                                             stop=False, skip_group_check=True)
                    if s == 0 and n == 2:
                        pe.wait_ge(um_diff.sem, um_diff.of(b))
                    for i, (w, m) in enumerate(((0, 0), (1, 0), (0, 1))):
                        if s == 0 and n == 0 and w == 0:
                            pe.wait_ge(um_first.sem, um_first.of(b, m + 1))
                        mm = nc.tensor.matmul(banks[n % 2][:], b13[w][:, s, cols], um[k][m][:, s, :], start=False,
                                              stop=(i == 2), skip_group_check=True)
                    mm.then_inc(done.sem, 1)

            def a2_product(b, c, k):
                if isinstance(b, int) and b == 0 and c == 0 and k == 0:
                    pe.wait_ge(w_lo_ready, 6)
                bank, split, lo_done, done = ((z_ps, z_split, z_lo_done, a2z_mm), (b_ps, b_split, b_lo_done, a2b_mm))[k]
                pe.wait_ge(lo_done.sem, lo_done.of(b, c + 1))
                for i, (w, m) in enumerate(TERMS):
                    mm = nc.tensor.matmul(bank[:], w2a2[w][:, c, D:D + ER], split[m][:, c, :],
                                          start=(c == 0 and i == 0), stop=(c == CHUNKS - 1 and i == 2),
                                          skip_group_check=True)
                if c == CHUNKS - 1:
                    mm.then_inc(done.sem, 1)

            def w2_product(b, c):
                if c == 0:
                    pe.wait_ge(v_part_done.sem, v_part_done.of(b, 1))
                for i, (w, m) in enumerate(TERMS):
                    nc.tensor.matmul(z_ps[:], w2a2[w][:, c, 0:D], z_split[m][:, c, :], start=(c == 0 and i == 0),
                                     stop=False, skip_group_check=True)

            def b2_product(b):
                pe.wait_ge(v_hi_done.sem, v_hi_done.of(b))
                pe.wait_ge(v_lo_done.sem, v_lo_done.of(b))
                for i, (w, m) in enumerate(TERMS):
                    mm = nc.tensor.matmul(z_ps[:], b2_split[w][:], v_split[m][:], start=False, stop=(i == 2),
                                          skip_group_check=True)
                mm.then_inc(o_t_mm.sem, 1)

            def tail(b, after_early=False, after_masks=False):
                pe.wait_ge(o_t_done.sem, o_t_done.of(b))
                if after_early:
                    pe.wait_ge(ktv_done.sem, ktv_done.of(b + 2))
                if after_masks:
                    pe.wait_ge(masks_done.sem, masks_done.of(b + 1))
                for t in range(TILES):
                    mm = nc.tensor.transpose(even_ps[:, t * P:(t + 1) * P], o_t[:, t * P:(t + 1) * P], ident[:])
                mm.then_inc(y_mm.sem, 1)

            def iteration(b, tail_too, late, early):
                first = not tail_too
                late_steps = late_half(b + 1, after_tail=not first, after_ratio=first, after_early=early) \
                    if late else iter(())
                early_steps = early_half(b + 2) if early else iter(())
                hidden(b, 0, first)
                if tail_too:
                    tail(b - 1, after_early=late, after_masks=not late)
                hidden(b, 1, first)
                next(late_steps, None)
                hidden(b, 2, first)
                next(late_steps, None)
                hidden(b, 3, first)
                hidden(b, 4, first)
                hidden(b, 5, first)
                next(late_steps, None)
                hidden(b, 6, first)
                next(late_steps, None)
                next(late_steps, None)
                hidden(b, 7, first)
                a2_product(b, 0, 0)
                a2_product(b, 0, 1)
                a2_product(b, 1, 1)
                next(late_steps, None)
                a2_product(b, 1, 0)
                next(early_steps, None)
                a2_product(b, 2, 0)
                a2_product(b, 2, 1)
                next(early_steps, None)
                a2_product(b, 3, 0)
                a2_product(b, 3, 1)
                next(early_steps, None)
                next(early_steps, None)
                w2_product(b, 0)
                w2_product(b, 1)
                next(late_steps, None)
                next(late_steps, None)
                next(late_steps, None)
                w2_product(b, 2)
                next(early_steps, None)
                w2_product(b, 3)
                next(early_steps, None)
                next(late_steps, None)
                next(early_steps, None)
                b2_product(b)

            first_early = early_ahead(0, even_ps, odd_ps, x_early=True)
            second_early = early_ahead(1, z_ps, b_ps, x_early=False)
            first_late = late_half(0)
            pe.wait_ge(qkv_w_in, QKV_W_IN)
            next(first_early)
            pe.wait_ge(ident_in, 16)
            next(first_early)
            next(first_early)
            next(first_early)
            next(first_early)
            next(first_early)
            pe.wait_ge(attn_w_in, ATTN_W_IN)
            next(second_early)
            next(second_early)
            next(first_late)
            next(first_late)
            next(second_early)
            next(second_early)
            next(second_early)
            next(first_late)
            next(second_early)
            pe.wait_ge(gate_w_ready, 1)
            pe.wait_ge(ident_bf_ready, 1)
            pe.wait_ge(w_lo_ready, 1)
            next(first_late)
            next(first_late)
            pe.wait_ge(w_lo_ready, 3)
            next(first_late)
            next(first_late)
            next(first_late)
            next(first_late)
            all_iterations(pe, iteration)
            pe.wait_ge(y_done.sem, y_done.of(BLOCKS - 2))
            tail(BLOCKS - 1)

        @block.scalar
        def _(sc):
            def early_xn_t(n, odd=odd_ps):
                sc.wait_ge(xn_t_mm.sem, xn_t_mm.of(n))
                nc.scalar.copy(xn_t[:], odd[:]).then_inc(xn_t_done.sem, 1)

            def early_ctx_hi(n):
                sc.wait_ge(ctx_loaded.sem, ctx_loaded.of(n))
                sc.wait_ge(kv_mm.sem, kv_mm.of(n - 1))
                nc.scalar.copy(ctx_split[0][:], ctx_in[:]).then_inc(ctx_hi_done.sem, 1)

            def early_q(n, even=even_ps):
                sc.wait_ge(q_mm.sem, q_mm.of(n))
                nc.scalar.activation(q_t[:], even[:], ACT.Identity, bias=bq_sb[:, 0:1]).then_inc(q_t_done.sem, 1)

            def early_exp(n):
                sc.wait_ge(o_shifted.sem, o_shifted.of(n))
                nc.scalar.activation(e_o[:], e_o[:], ACT.Exp).then_inc(o_exp.sem, 1)

            def late_heads_t(n):
                sc.wait_ge(heads_t_mm.sem, heads_t_mm.of(n))
                nc.scalar.copy(heads_t[:], odd_ps[:]).then_inc(heads_t_done.sem, 1)

            def late_tok_t(n):
                sc.wait_ge(tok_t_mm.sem, tok_t_mm.of(n))
                nc.scalar.copy(tok_t[:], odd_ps[:]).then_inc(tok_t_done.sem, 1)

            def late_t_hi(n):
                nc.scalar.copy(t_split[0][:], odd_ps[:]).then_inc(t_hi_done.sem, 1)

            def late_gap(n):
                sc.wait_ge(gap_done.sem, gap_done.of(n))
                nc.scalar.activation(e_gap[:], gap[:], ACT.Exp).then_inc(e_gap_done.sem, 1)

            def late_u_hi(n, s):
                sc.wait_ge(u_mm.sem, u_mm.of(n, s + 1))
                nc.scalar.copy(u_hi[:, s, :], (odd_ps, even_ps)[s][:]).then_inc(u_hi_done.sem, 1)

            def late_spread(n, k):
                done = (onehot_done, onehot_diff)[k]
                sc.wait_ge(done.sem, done.of(n))
                src = onehot[:, 2 * k].unsqueeze(3).to_broadcast([P, TILES, EXPERTS, RANK])
                nc.scalar.copy(spread[:, k], src).then_inc(spread_done.sem, 1)

            def late_wide_ratio(n):
                sc.wait_ge(e_gap_done.sem, e_gap_done.of(n))
                nc.scalar.copy(wide_ratio[:], e_gap[:].unsqueeze(2).to_broadcast([P, TILES, P]))\
                    .then_inc(wide_ratio_done.sem, 1)

            def late_mask(n, k, first=False):
                sc.wait_ge(masks_mm.sem, masks_mm.of(n, k + 1))
                if not first:
                    sc.wait_ge(v_part_done.sem, v_part_done.of(n - 1, k + 1))
                nc.scalar.copy(masks[:, k, :], (odd_ps, even_ps)[k][:]).then_inc(masks_done.sem, 1)

            def late_ratio(n):
                sc.wait_ge(ratio_mm.sem, ratio_mm.of(n))
                nc.scalar.copy(ratio[:], odd_ps[:]).then_inc(ratio_done.sem, 1)

            def residual(b, first):
                sc.wait_ge(x1_done.sem, x1_done.of(b))
                if not first:
                    sc.wait_ge(y_done.sem, y_done.of(b - 1))
                nc.scalar.copy(res[:], x1[:]).then_inc(res_done.sem, 1)

            def silu_step(b, n):
                sc.wait_ge(h1_mm.sem, h1_mm.of(b, n + 1))
                nc.scalar.activation(silu[:, n % SILU_RING, :], h1_ps[n % 2][:], ACT.Silu).then_inc(silu_done.sem, 1)

            def b_high(b, c):
                sc.wait_ge(scaled_done.sem, scaled_done.of(b, c + 1))
                nc.scalar.copy(b_split[0][:, c, :], scaled[:, c, :]).then_inc(b_hi_done.sem, 1)

            def z_high(b, c):
                sc.wait_ge(total_done.sem, total_done.of(b, c + 1))
                nc.scalar.copy(z_split[0][:, c, :], total[:, c, :]).then_inc(z_hi_done.sem, 1)

            def v_high(b):
                sc.wait_ge(v_done.sem, v_done.of(b))
                nc.scalar.copy(v_split[0][:], v[:]).then_inc(v_hi_done.sem, 1)

            def output_t(b):
                sc.wait_ge(o_t_mm.sem, o_t_mm.of(b))
                nc.scalar.copy(o_t[:], z_ps[:]).then_inc(o_t_done.sem, 1)

            def iteration(b, tail_too, late, early):
                if tail_too:
                    output_t(b - 1)
                silu_step(b, 0)
                residual(b, first=not tail_too)
                silu_step(b, 1)
                if late:
                    late_heads_t(b + 1)
                silu_step(b, 2)
                silu_step(b, 3)
                silu_step(b, 4)
                z_high(b, 0)
                b_high(b, 0)
                b_high(b, 1)
                silu_step(b, 5)
                z_high(b, 1)
                if late:
                    late_tok_t(b + 1)
                    late_t_hi(b + 1)
                if early:
                    early_ctx_hi(b + 2)
                silu_step(b, 6)
                silu_step(b, 7)
                if late:
                    late_u_hi(b + 1, 0)
                b_high(b, 2)
                z_high(b, 2)
                b_high(b, 3)
                if late:
                    late_u_hi(b + 1, 1)
                z_high(b, 3)
                if early:
                    early_xn_t(b + 2)
                if late:
                    late_gap(b + 1)
                    late_spread(b + 1, 0)
                    late_spread(b + 1, 1)
                    late_wide_ratio(b + 1)
                if early:
                    early_q(b + 2)
                v_high(b)
                if late:
                    late_mask(b + 1, 0)
                    late_mask(b + 1, 1)
                    late_ratio(b + 1)
                if early:
                    early_exp(b + 2)

            sc.dma_start(ctx_in[:], ctx_t[:, 0:BLK]).then_inc(ctx_loaded.sem, 16)
            sc.dma_start(bkv_sb[:], wkv_b.partition_broadcast(P)).then_inc(qkv_w_in, 16)
            sc.dma_start(bq_sb[:], wq_b).then_inc(qkv_w_in, 16)
            sc.dma_start(bo_sb[:], wo_b.partition_broadcast(P)).then_inc(attn_w_in, 16)
            sc.dma_start(nw_raw[:], norm_w).then_inc(lora_w_in, 16)
            early_xn_t(0, h1_ps[0])
            sc.dma_start(gate_raw[:], gate_t).then_inc(lora_w_in, 16)
            sc.wait_ge(qkv_w_in, QKV_W_IN)
            early_q(0, h1_ps[1])
            sc.dma_start(a13_raw[:, 0, :], a1_t).then_inc(lora_w_in, 16)
            early_exp(0)
            sc.dma_start(a13_raw[:, 1, :], a3_t).then_inc(lora_w_in, 16)
            sc.dma_start(b13_raw[:, 0, :], b1).then_inc(hidden_w_in, 16)
            sc.dma_start(b13_raw[:, 1, :], b3).then_inc(hidden_w_in, 16)
            sc.dma_start(iota_sb[:], expert_iota.partition_broadcast(P)).then_inc(lora_w_in, 16)
            late_heads_t(0)
            early_xn_t(1, h1_ps[0])
            sc.wait_ge(nw_ready, 1)
            sc.wait_ge(lora_w_in, LORA_W_IN)
            nc.scalar.activation(a13[0][:], a13_raw[:], ACT.Identity, scale=nw_sb[:, 0:1]).then_inc(w_hi_ready, 1)
            early_q(1, h1_ps[1])
            sc.wait_ge(hidden_w_in, HIDDEN_W_IN)
            nc.scalar.activation(w13[0][:], w13_raw[:], ACT.Identity, scale=nw_sb[:, 0:1]).then_inc(w_hi_ready, 1)
            nc.scalar.activation(b13[0][:], b13_raw[:], ACT.Identity, scale=LORA_SCALE).then_inc(w_hi_ready, 1)
            sc.wait_ge(down_w_in, DOWN_W_IN)
            nc.scalar.copy(w2a2[0][:], w2a2_raw[:]).then_inc(w_hi_ready, 1)
            nc.scalar.activation(b2_split[0][:], b2_raw[:], ACT.Identity, scale=LORA_SCALE).then_inc(w_hi_ready, 1)
            late_tok_t(0)
            late_t_hi(0)
            late_u_hi(0, 0)
            nc.scalar.copy(wkv_split[0][:], wkv_sb[:]).then_inc(w_hi_ready, 1)
            late_u_hi(0, 1)
            late_spread(0, 0)
            late_spread(0, 1)
            late_gap(0)
            late_mask(0, 0, first=True)
            late_mask(0, 1, first=True)
            late_wide_ratio(0)
            early_exp(1)
            late_ratio(0)
            all_iterations(sc, iteration)
            output_t(BLOCKS - 1)

        @block.vector
        def _(ve):
            def normalise(dst, src, mean_var, rs, rstd_sig, n, done):
                ve.wait_ge(rstd_sig.sem, rstd_sig.of(n))
                for t in range(TILES):
                    op = nc.vector.tensor_scalar(dst[:, t, :], src[:, t, :], mean_var[:, t, 0:1], rs[:, t:t + 1],
                                                 ALU.subtract, ALU.mult)
                op.then_inc(done.sem, 1)

            def moments(src, st, mean_var, st_sig, mv_sig, n):
                for t in range(TILES):
                    op = nc.vector.bn_stats(st[:, t, :], src[:, t, :])
                op.then_inc(st_sig.sem, 1)
                ve.wait_ge(st_sig.sem, st_sig.of(n))
                nc.vector.memset(carrier[:], 0.0)
                for t in range(TILES):
                    op = nc.vector.bn_aggr(mean_var[:, t, :], st[:, t, :])
                op.then_inc(mv_sig.sem, 1)

            def early_moments(n):
                ve.wait_ge(x_loaded.sem, x_loaded.of(n))
                moments(x_in, stats, mv, stats_done, mv_done, n)

            def early_xn(n):
                normalise(xn, x_in, mv, rstd, rstd_done, n, xn_done)

            def early_kv(n, half, banks=(even_ps, odd_ps)):
                ve.wait_ge(kv_mm.sem, kv_mm.of(n, half + 1))
                nc.vector.tensor_tensor(kv[:, 2 * half:2 * half + 2, :],
                                        banks[half][:].rearrange("p (t d) -> p t d", t=2),
                                        bkv_sb[:].unsqueeze(1).to_broadcast([P, 2, 2 * P]), ALU.add)\
                    .then_inc(kv_done.sem, 1)

            def early_ktv(n, even=even_ps):
                ve.wait_ge(ktv_mm.sem, ktv_mm.of(n))
                nc.vector.tensor_tensor(ktv[:], tile4(even), mask_sb[:].unsqueeze(1).to_broadcast([P, TILES, P]),
                                        ALU.mult).then_inc(ktv_done.sem, 1)

            def early_shift(n, odd=odd_ps, first=False):
                ve.wait_ge(o_mm.sem, o_mm.of(n))
                o = odd[:].rearrange("p (g k) -> p g k", k=DK)
                nc.vector.tensor_reduce(top_o[:], o, AX_X, ALU.max).then_inc(top_o_done.sem, 1)
                ve.wait_ge(top_o_done.sem, top_o_done.of(n))
                if not first:
                    ve.wait_ge(heads_done.sem, heads_done.of(n - 1))
                nc.vector.tensor_tensor(e_o[:], o, top_o[:].unsqueeze(2).to_broadcast([P, TILES * HEADS, DK]),
                                        ALU.subtract).then_inc(o_shifted.sem, 1)

            def late_sum(n):
                ve.wait_ge(o_exp.sem, o_exp.of(n))
                nc.vector.tensor_reduce(sum_o[:], e_o[:], AX_X, ALU.add).then_inc(sum_o_done.sem, 1)
                ve.wait_ge(sum_o_done.sem, sum_o_done.of(n))
                nc.vector.reciprocal(rec_o[:], sum_o[:]).then_inc(rec_o_done.sem, 1)

            def late_x1(n, first=False):
                ve.wait_ge(wo_mm.sem, wo_mm.of(n))
                ve.wait_ge(x_bias_done.sem, x_bias_done.of(n))
                if not first:
                    ve.wait_ge(res_done.sem, res_done.of(n - 1))
                nc.vector.tensor_tensor(x1[:], tile4(even_ps), x_bias[:], ALU.add).then_inc(x1_done.sem, 1)

            def late_moments(n):
                ve.wait_ge(x1_done.sem, x1_done.of(n))
                moments(x1, stats2, mv2, stats2_done, mv2_done, n)

            def late_tok(n):
                normalise(tok, x1, mv2, rstd2, rstd2_done, n, tok_done)

            def late_t_lo(n):
                ve.wait_ge(tok_t_done.sem, tok_t_done.of(n))
                ve.wait_ge(t_hi_done.sem, t_hi_done.of(n))
                nc.vector.tensor_tensor(t_split[1][:], tok_t[:], as_f32(t_split[0][:]), ALU.subtract)\
                    .then_inc(t_lo_done.sem, 1)

            def late_logits(n):
                ve.wait_ge(logits_mm.sem, logits_mm.of(n))
                nc.vector.tensor_copy(logits[:], tile4(even_ps)[:, :, 0:EXPERTS]).then_inc(logits_done.sem, 1)

            def late_gate(n):
                ve.wait_ge(logits_done.sem, logits_done.of(n))
                nc.vector.memset(carrier[:], 0.0)
                for t in range(TILES):
                    op = nc.vector.max(top_l[:, t, :], logits[:, t, :])
                op.then_inc(top_l_done.sem, 1)
                ve.wait_ge(top_l_done.sem, top_l_done.of(n))
                nc.vector.tensor_tensor(gap[:], top_l[:, :, 1], top_l[:, :, 0], ALU.subtract).then_inc(gap_done.sem, 1)

            def late_onehots(n):
                for t in range(TILES):
                    op = nc.vector.max_index(top_i[:, t, :], top_l[:, t, :], logits[:, t, :])
                op.then_inc(top_i_done.sem, 1)
                ve.wait_ge(top_i_done.sem, top_i_done.of(n))
                for k in range(TOP):
                    op = nc.vector.tensor_tensor(onehot[:, k], iota_sb[:].unsqueeze(1).to_broadcast([P, TILES, EXPERTS]),
                                                 top_i[:, :, k:k + 1].to_broadcast([P, TILES, EXPERTS]), ALU.is_equal)
                op.then_inc(onehot_done.sem, 1)
                ve.wait_ge(onehot_done.sem, onehot_done.of(n))
                nc.vector.tensor_tensor(onehot[:, 2], onehot[:, 1], onehot[:, 0], ALU.subtract)\
                    .then_inc(onehot_diff.sem, 1)

            def late_weight(n):
                ve.wait_ge(e_gap_done.sem, e_gap_done.of(n))
                nc.vector.tensor_scalar(den[:], e_gap[:], 1.0, None, ALU.add).then_inc(den_done.sem, 1)
                ve.wait_ge(den_done.sem, den_done.of(n))
                nc.vector.reciprocal(w_new[:], den[:]).then_inc(w0_done.sem, 1)

            def late_u_lo(n, s):
                ve.wait_ge(u_hi_done.sem, u_hi_done.of(n, s + 1))
                nc.vector.tensor_tensor(u_lo[:, s, :], (odd_ps, even_ps)[s][:], as_f32(u_hi[:, s, :]), ALU.subtract)\
                    .then_inc(u_lo_done.sem, 1)

            def late_um_first(n, part):
                if part == 0:
                    ve.wait_ge(masks_done.sem, masks_done.of(n, 1))
                    ve.wait_ge(u_lo_done.sem, u_lo_done.of(n))
                nc.vector.tensor_tensor(um[0][part][:], as_f32((u_hi, u_lo)[part][:]),
                                        masks[:, 0:1, :].to_broadcast([P, 2, BLK]), ALU.mult)\
                    .then_inc(um_first.sem, 1)

            def hand_over(b, first):
                ve.wait_ge(w0_done.sem, w0_done.of(b))
                if not first:
                    ve.wait_ge(y_done.sem, y_done.of(b - 1))
                nc.vector.tensor_copy(w_use[:], w_new[:]).then_inc(handed_over.sem, 1)

            def act_step(b, n):
                c, k = STEPS[n]
                ve.wait_ge(silu_done.sem, silu_done.of(b, n + 1))
                ve.wait_ge(h3_mm.sem, h3_mm.of(b, n + 1))
                dst = act_first[:, c, :] if k == 0 else act_second[:, c % 2, :]
                nc.vector.tensor_tensor(dst, silu[:, n % SILU_RING, :], h3_ps[n % 2][:], ALU.mult)\
                    .then_inc(act_done.sem, 1)

            def last_b(b, c):
                ve.wait_ge(act_done.sem, act_done.of(b, STEPS.index((c, 1)) + 1))
                ve.wait_ge(scaled_done.sem, scaled_done.of(b, c))
                nc.vector.tensor_tensor(scaled[:, c, :], act_second[:, c % 2, :], ratio[:], ALU.mult)\
                    .then_inc(scaled_done.sem, 1)

            def last_b_low(b, c):
                ve.wait_ge(b_lo_done.sem, b_lo_done.of(b, c))
                ve.wait_ge(b_hi_done.sem, b_hi_done.of(b, c + 1))
                nc.vector.tensor_tensor(b_split[1][:, c, :], scaled[:, c, :], as_f32(b_split[0][:, c, :]), ALU.subtract)\
                    .then_inc(b_lo_done.sem, 1)

            def total_step(b, c):
                ve.wait_ge(scaled_done.sem, scaled_done.of(b, c + 1))
                nc.vector.tensor_tensor(total[:, c, :], act_first[:, c, :], scaled[:, c, :], ALU.add)\
                    .then_inc(total_done.sem, 1)

            def total_low(b, c):
                ve.wait_ge(z_hi_done.sem, z_hi_done.of(b, c + 1))
                nc.vector.tensor_tensor(z_split[1][:, c, :], total[:, c, :], as_f32(z_split[0][:, c, :]), ALU.subtract)\
                    .then_inc(z_lo_done.sem, 1)

            def v_part(b, k):
                done = (a2z_mm, a2b_mm)[k]
                ve.wait_ge(done.sem, done.of(b))
                nc.vector.tensor_tensor(v_parts[:, k, :], (z_ps, b_ps)[k][:], masks[:, k, :], ALU.mult)\
                    .then_inc(v_part_done.sem, 1)

            def v_sum(b):
                ve.wait_ge(v_part_done.sem, v_part_done.of(b))
                nc.vector.tensor_tensor(v[:], v_parts[:, 0, :], v_parts[:, 1, :], ALU.add).then_inc(v_done.sem, 1)

            def v_low(b):
                ve.wait_ge(v_hi_done.sem, v_hi_done.of(b))
                nc.vector.tensor_tensor(v_split[1][:], v[:], as_f32(v_split[0][:]), ALU.subtract)\
                    .then_inc(v_lo_done.sem, 1)

            def finish(b):
                ve.wait_ge(y_mm.sem, y_mm.of(b))
                ve.wait_ge(res_done.sem, res_done.of(b))
                ve.wait_ge(handed_over.sem, handed_over.of(b))
                ve.wait_ge(stored.sem, stored.of(b))
                for t in range(TILES):
                    op = nc.vector.scalar_tensor_tensor(out=y[:, t, :], in0=even_ps[:, t * P:(t + 1) * P],
                                                        scalar=w_use[:, t:t + 1], in1=res[:, t, :], op0=ALU.mult,
                                                        op1=ALU.add)
                op.then_inc(y_done.sem, 1)

            def iteration(b, tail_too, late, early):
                if late:
                    late_sum(b + 1)
                if tail_too:
                    finish(b - 1)
                hand_over(b, first=not tail_too)
                act_step(b, 0)
                act_step(b, 1)
                act_step(b, 2)
                if late:
                    late_x1(b + 1)
                    late_moments(b + 1)
                act_step(b, 3)
                total_step(b, 0)
                if late:
                    late_tok(b + 1)
                total_low(b, 0)
                total_step(b, 1)
                act_step(b, 4)
                if early:
                    early_moments(b + 2)
                act_step(b, 5)
                if late:
                    late_t_lo(b + 1)
                total_low(b, 1)
                act_step(b, 6)
                if late:
                    late_logits(b + 1)
                if early:
                    early_xn(b + 2)
                act_step(b, 7)
                total_step(b, 2)
                if not late:
                    last_b(b, CHUNKS - 1)
                if late:
                    late_u_lo(b + 1, 0)
                total_low(b, 2)
                total_step(b, 3)
                if late:
                    late_u_lo(b + 1, 1)
                if not late:
                    last_b_low(b, CHUNKS - 1)
                total_low(b, 3)
                if late:
                    late_gate(b + 1)
                    late_onehots(b + 1)
                if early:
                    early_kv(b + 2, 0)
                v_part(b, 0)
                v_part(b, 1)
                if early:
                    early_kv(b + 2, 1)
                v_sum(b)
                v_low(b)
                if late:
                    late_um_first(b + 1, 0)
                    late_um_first(b + 1, 1)
                if early:
                    early_ktv(b + 2)
                    early_shift(b + 2)
                if late:
                    late_weight(b + 1)

            nc.vector.memset(gate_sb[:], 0.0).then_inc(gate_zero, 1)
            nc.vector.memset(y[:], 0.0).then_inc(stored.sem, stored.per_block)
            def low(i, split, raw, scale):
                ve.wait_ge(w_hi_ready, i + 1)
                if scale is None:
                    op = nc.vector.tensor_tensor(split[1][:], raw[:], as_f32(split[0][:]), ALU.subtract)
                else:
                    op = nc.vector.scalar_tensor_tensor(out=split[1][:], in0=raw[:], scalar=scale,
                                                        in1=as_f32(split[0][:]), op0=ALU.mult, op1=ALU.subtract)
                op.then_inc(w_lo_ready, 1)

            early_moments(0)
            ve.wait_ge(ident_in, 16)
            nc.vector.tensor_copy(ident_bf[:], ident[:]).then_inc(ident_bf_ready, 1)
            early_xn(0)
            ve.wait_ge(qkv_w_in, QKV_W_IN)
            early_kv(0, 0, h3_ps)
            early_kv(0, 1, h3_ps)
            ve.wait_ge(attn_w_in, ATTN_W_IN)
            early_ktv(0)
            early_shift(0, first=True)
            late_sum(0)
            early_moments(1)
            early_kv(1, 0, h3_ps)
            early_xn(1)
            early_kv(1, 1, h3_ps)
            ve.wait_ge(lora_w_in, LORA_W_IN)
            nc.vector.tensor_scalar(nw_sb[:], nw_raw[:], (1.0 + RMS_EPS) ** -0.5, None, ALU.mult).then_inc(nw_ready, 1)
            late_x1(0, first=True)
            late_moments(0)
            ve.wait_ge(gate_zero, 1)
            ve.wait_ge(nw_ready, 1)
            nc.vector.tensor_scalar(gate_sb[:, 0:EXPERTS], gate_raw[:], nw_sb[:, 0:1], None, ALU.mult)\
                .then_inc(gate_w_ready, 1)
            low(0, a13, a13_raw, nw_sb[:, 0:1])
            early_ktv(1, z_ps)
            late_tok(0)
            low(1, w13, w13_raw, nw_sb[:, 0:1])
            late_t_lo(0)
            low(2, b13, b13_raw, LORA_SCALE)
            late_logits(0)
            late_gate(0)
            late_u_lo(0, 0)
            low(3, w2a2, w2a2_raw, None)
            low(4, b2_split, b2_raw, LORA_SCALE)
            low(5, wkv_split, wkv_sb, None)
            early_shift(1, b_ps)
            late_onehots(0)
            late_u_lo(0, 1)
            late_um_first(0, 0)
            late_weight(0)
            late_um_first(0, 1)
            all_iterations(ve, iteration)
            finish(BLOCKS - 1)

        @block.gpsimd
        def _(pool):
            def inverse_root(src, var_out, rs, mv_sig, var_sig, rstd_sig, n, eps):
                pool.wait_ge(mv_sig.sem, mv_sig.of(n))
                nc.gpsimd.tensor_tensor(var_out[:], src[:, :, 1], eps[:], ALU.add).then_inc(var_sig.sem, 1)
                pool.wait_ge(var_sig.sem, var_sig.of(n))
                nc.gpsimd.tensor_tensor(rs[:], var_out[:], minus_half[:], ALU.pow).then_inc(rstd_sig.sem, 1)

            def early_rstd(n):
                inverse_root(mv, var_eps, rstd, mv_done, var_done, rstd_done, n, eps_ln)

            def early_ctx_lo(n):
                pool.wait_ge(ctx_hi_done.sem, ctx_hi_done.of(n - AHEAD))
                nc.gpsimd.tensor_tensor(ctx_split[1][:], ctx_in[:], as_f32(ctx_split[0][:]), ALU.subtract)\
                    .then_inc(ctx_lo_done.sem, 1)

            def early_bias(n, first=False):
                pool.wait_ge(x_loaded.sem, x_loaded.of(n))
                if not first:
                    pool.wait_ge(x1_done.sem, x1_done.of(n - 1))
                nc.gpsimd.tensor_tensor(x_bias[:], x_in[:], bo_sb[:].unsqueeze(1).to_broadcast([P, TILES, D]), ALU.add)\
                    .then_inc(x_bias_done.sem, 1)

            def late_heads(n):
                pool.wait_ge(rec_o_done.sem, rec_o_done.of(n))
                nc.gpsimd.tensor_tensor(heads[:].rearrange("p t (h k) -> p (t h) k", k=DK), e_o[:],
                                        rec_o[:].unsqueeze(2).to_broadcast([P, TILES * HEADS, DK]), ALU.mult)\
                    .then_inc(heads_done.sem, 1)

            def late_rstd(n):
                inverse_root(mv2, var_eps2, rstd2, mv2_done, var2_done, rstd2_done, n, eps_rms)

            def late_um_diff(n):
                pool.wait_ge(masks_done.sem, masks_done.of(n))
                pool.wait_ge(u_lo_done.sem, u_lo_done.of(n))
                mask = masks[:, 1:2, :].to_broadcast([P, 2, BLK])
                nc.gpsimd.tensor_tensor(um[1][0][:], as_f32(u_hi[:]), mask, ALU.mult)
                nc.gpsimd.tensor_tensor(um[1][1][:], as_f32(u_lo[:]), mask, ALU.mult).then_inc(um_diff.sem, 1)

            def scale_step(b, c):
                if c == 0:
                    pool.wait_ge(ratio_done.sem, ratio_done.of(b))
                n = STEPS.index((c, 1))
                pool.wait_ge(act_done.sem, act_done.of(b, n + 1))
                nc.gpsimd.tensor_tensor(scaled[:, c, :], act_second[:, c % 2, :], ratio[:], ALU.mult)\
                    .then_inc(scaled_done.sem, 1)

            def scaled_low(b, c):
                pool.wait_ge(b_hi_done.sem, b_hi_done.of(b, c + 1))
                nc.gpsimd.tensor_tensor(b_split[1][:, c, :], scaled[:, c, :], as_f32(b_split[0][:, c, :]), ALU.subtract)\
                    .then_inc(b_lo_done.sem, 1)

            def iteration(b, tail_too, late, early):
                if late:
                    late_heads(b + 1)
                scale_step(b, 0)
                if late:
                    late_rstd(b + 1)
                scale_step(b, 1)
                scaled_low(b, 0)
                scaled_low(b, 1)
                if early:
                    early_rstd(b + 2)
                    early_ctx_lo(b + 2)
                scale_step(b, 2)
                if late:
                    scale_step(b, 3)
                scaled_low(b, 2)
                if late:
                    scaled_low(b, 3)
                    late_um_diff(b + 1)
                if early:
                    early_bias(b + 2)

            nc.gpsimd.memset(eps_ln[:], LN_EPS)
            nc.gpsimd.memset(eps_rms[:], LN_EPS * RMS_EPS / (1.0 + RMS_EPS))
            nc.gpsimd.memset(minus_half[:], -0.5).then_inc(const_pool, 1)
            pool.wait_ge(const_pool, 1)
            early_rstd(0)
            pool.wait_ge(attn_w_in, ATTN_W_IN)
            early_bias(0, first=True)
            late_heads(0)
            early_rstd(1)
            late_rstd(0)
            late_um_diff(0)
            early_bias(1)
            all_iterations(pool, iteration)


_OUT = "out_dram"


def kernel(**inputs):
    import numpy as np
    import concourse.bacc as bacc
    from concourse.bass_utils import run_bass_kernel_spmd

    a = {k: np.asarray(v) for k, v in inputs.items()}
    at, ff = (lambda n: a["L0_xattn_" + n]), (lambda n: a["L0_ffn_" + n])

    def heads_side_by_side(w):
        return w.transpose(1, 0, 2).reshape(D, HEADS * DK)

    arrays = {
        "x": a["x"].transpose(1, 0, 2).reshape(SEQ, BATCH * D),
        "ctx_t": a["ctx_1024"].transpose(2, 0, 1).reshape(D, BATCH * SEQ),
        "wq": heads_side_by_side(at("wq_w")),
        "wq_b": at("wq_b").reshape(HEADS * DK, 1),
        "wkv": np.concatenate([heads_side_by_side(at("wk_w")), heads_side_by_side(at("wv_w"))], axis=1),
        "wkv_b": np.concatenate([at("wk_b").reshape(-1), at("wv_b").reshape(-1)]),
        "wo_t": at("wo_w").T,
        "wo_b": at("wo_b"),
        "norm_w": ff("norm_w").reshape(D, 1),
        "gate_t": ff("gate_w").T,
        "w1_t": ff("w1").T, "w3_t": ff("w3").T, "w2_t": ff("w2").T,
        "a1_t": ff("a1").reshape(ER, D).T, "a3_t": ff("a3").reshape(ER, D).T,
        "a2_t": ff("a2").reshape(ER, FF).T,
        "b1": ff("b1").transpose(0, 2, 1).reshape(ER, FF), "b3": ff("b3").transpose(0, 2, 1).reshape(ER, FF),
        "b2": ff("b2").transpose(0, 2, 1).reshape(ER, D),
        "head_mask": np.kron(np.eye(HEADS), np.ones((DK, DK))).astype(np.float32) * np.float32(DK ** -0.5),
        "identity": np.eye(P, dtype=np.float32),
        "expert_iota": np.arange(EXPERTS, dtype=np.float32),
    }
    nc = bacc.Bacc("TRN2", target_bir_lowering=False, num_devices=1)
    feed, args = {}, []
    for name, value in arrays.items():
        value = np.ascontiguousarray(value)
        feed[f"in_{name}_dram"] = value
        args.append(nc.dram_tensor(f"in_{name}_dram", value.shape, mybir.dt.from_np(value.dtype), kind="ExternalInput").ap())
    args.append(nc.dram_tensor(_OUT, (SEQ, BATCH * D), F32, kind="ExternalOutput").ap())
    build_program(nc, *args)
    r = run_bass_kernel_spmd(nc, [feed], core_ids=[0])
    return r.results[0][_OUT].reshape(SEQ, BATCH, D).transpose(1, 0, 2)
```
